# Optimizing a Trainium2 kernel written in Bass

```python
import numpy as np
import jax
import jax.numpy as jnp

def _softmax(x, axis=-1):
    return jax.nn.softmax(x, axis=axis)

def _gelu(x):
    return jax.nn.gelu(x, approximate=True)

def _silu(x):
    return jax.nn.silu(x)

def _sigmoid(x):
    return jax.nn.sigmoid(x)

def _layernorm(x, axis=-1, eps=1e-05):
    m = jnp.mean(x, axis=axis, keepdims=True)
    v = jnp.var(x, axis=axis, keepdims=True)
    return (x - m) / jnp.sqrt(v + eps)

def _scatter_add(tgt, idx, src, axis=0):
    return tgt.at[idx].add(src)

def _segment_sum(src, seg, n):
    return jax.ops.segment_sum(src, seg, n)
kernel_name = 'mk_adj_resnorm_d4_adj_r2_f75899'

def setup_inputs(seed: int=0):
    np.random.seed(seed)
    _w = jnp.asarray

    def _rec_inputs():
        import jax
        import jax.numpy as jnp
        _gk = jax.random.key(seed)
        x = 7.22e-05 + 1 * jax.random.normal(jax.random.fold_in(_gk, 1), (16, 512, 256), jnp.float32)
        _a = jax.random.bernoulli(jax.random.fold_in(_gk, 2), 0.03125, (512, 512))
        _af = _a.astype(jnp.float32)
        adj = _af
        return (x, adj)
    x, adj = _rec_inputs()

    def _L0_gnn_setup():
        import jax, jax.numpy as jnp
        import numpy as np
        B, N, D = (8, 1024, 256)
        key = jax.random.key(seed)
        k1, k2, k3, k4, k5 = jax.random.split(key, 5)
        neuron_states = jax.random.normal(k1, (B, N, D), dtype=jnp.float32)
        adjacency = jax.random.randint(k2, (N, N), 0, 2).astype(jnp.float32)
        scale = 1.0 / np.sqrt(D)
        Wq = jax.random.normal(k3, (D, D), dtype=jnp.float32) * scale
        Wk = jax.random.normal(k4, (D, D), dtype=jnp.float32) * scale
        Wv = jax.random.normal(k5, (D, D), dtype=jnp.float32) * scale
        return {'neuron_states': neuron_states, 'adjacency': adjacency, 'Wq': Wq, 'Wk': Wk, 'Wv': Wv}
    _L0_gnn_all = _L0_gnn_setup()
    _L0_gnn_in = {k: v for k, v in _L0_gnn_all.items() if k in ('Wq', 'Wk', 'Wv')}
    del _L0_gnn_all

    def _L1_gnn_setup():
        import jax, jax.numpy as jnp
        import numpy as np
        B, N, F_IN, F_OUT = (16, 1024, 256, 256)
        key = jax.random.key(seed)
        k1, k2, k3 = jax.random.split(key, 3)
        x = jax.random.normal(k1, (B, N, F_IN), dtype=jnp.float32)
        adj = jax.random.uniform(k2, (N, N), dtype=jnp.float32)
        bound = np.sqrt(6.0 / F_OUT)
        weight = jax.random.uniform(k3, (F_IN, F_OUT), dtype=jnp.float32, minval=-bound, maxval=bound)
        bias = jnp.zeros((F_OUT,), dtype=jnp.float32)
        return {'x': x, 'adj': adj, 'weight': weight, 'bias': bias}
    _L1_gnn_all = _L1_gnn_setup()
    _L1_gnn_in = {k: v for k, v in _L1_gnn_all.items() if k in ('weight', 'bias')}
    del _L1_gnn_all

    def _L2_gnn_setup():
        import jax, jax.numpy as jnp
        import numpy as np
        B, N, D, T = (64, 128, 256, 3)

        def _lin(v, W, b):
            return jnp.einsum('...i,oi->...o', v, W) + b
        key = jax.random.key(seed)
        ks = jax.random.split(key, 12)
        s2 = 1.0 / np.sqrt(2 * D)
        s1 = 1.0 / np.sqrt(D)
        return {'x': jax.random.normal(ks[0], (B, N, D), jnp.float32), 'in_mat': jax.random.uniform(ks[1], (N, N), jnp.float32) / N, 'out_mat': jax.random.uniform(ks[2], (N, N), jnp.float32) / N, 'w3_w': jax.random.normal(ks[3], (D, 2 * D), jnp.float32) * s2, 'w3_b': jnp.zeros((D,), jnp.float32), 'u3_w': jax.random.normal(ks[4], (D, D), jnp.float32) * s1, 'u3_b': jnp.zeros((D,), jnp.float32), 'w4_w': jax.random.normal(ks[5], (D, 2 * D), jnp.float32) * s2, 'w4_b': jnp.zeros((D,), jnp.float32), 'w5_w': jax.random.normal(ks[6], (D, 2 * D), jnp.float32) * s2, 'w5_b': jnp.zeros((D,), jnp.float32), 'u5_w': jax.random.normal(ks[7], (D, D), jnp.float32) * s1, 'u5_b': jnp.zeros((D,), jnp.float32)}
    _L2_gnn_all = _L2_gnn_setup()
    _L2_gnn_in = {k: v for k, v in _L2_gnn_all.items() if k in ('w3_w', 'w3_b', 'u3_w', 'u3_b', 'w4_w', 'w4_b', 'w5_w', 'w5_b', 'u5_w', 'u5_b')}
    del _L2_gnn_all

    def _L3_gnn_setup():
        import jax, jax.numpy as jnp
        import numpy as np
        B, N, D, H = (4, 1024, 256, 8)
        HD = D // H
        key = jax.random.key(seed)
        ks = jax.random.split(key, 10)
        x = jax.random.normal(ks[0], (B, N, D), dtype=jnp.float32)
        adj = (jax.random.uniform(ks[1], (N, N)) < 0.1).astype(jnp.float32)
        s = 1.0 / np.sqrt(D)
        Wq = jax.random.normal(ks[2], (D, D), dtype=jnp.float32) * s
        Wk = jax.random.normal(ks[3], (D, D), dtype=jnp.float32) * s
        Wv = jax.random.normal(ks[4], (D, D), dtype=jnp.float32) * s
        Wo = jax.random.normal(ks[5], (D, D), dtype=jnp.float32) * s
        bq = jnp.zeros((D,), jnp.float32)
        bk = jnp.zeros((D,), jnp.float32)
        bv = jnp.zeros((D,), jnp.float32)
        bo = jnp.zeros((D,), jnp.float32)
        return {'x': x, 'adj': adj, 'Wq': Wq, 'bq': bq, 'Wk': Wk, 'bk': bk, 'Wv': Wv, 'bv': bv, 'Wo': Wo, 'bo': bo}
    _L3_gnn_all = _L3_gnn_setup()
    _L3_gnn_in = {k: v for k, v in _L3_gnn_all.items() if k in ('Wq', 'bq', 'Wk', 'bk', 'Wv', 'bv', 'Wo', 'bo')}
    del _L3_gnn_all
    return {'x': x, 'adj': adj, 'L0_gnn_Wq': _L0_gnn_in['Wq'], 'L0_gnn_Wk': _L0_gnn_in['Wk'], 'L0_gnn_Wv': _L0_gnn_in['Wv'], 'L1_gnn_weight': _L1_gnn_in['weight'], 'L1_gnn_bias': _L1_gnn_in['bias'], 'L2_gnn_w3_w': _L2_gnn_in['w3_w'], 'L2_gnn_w3_b': _L2_gnn_in['w3_b'], 'L2_gnn_u3_w': _L2_gnn_in['u3_w'], 'L2_gnn_u3_b': _L2_gnn_in['u3_b'], 'L2_gnn_w4_w': _L2_gnn_in['w4_w'], 'L2_gnn_w4_b': _L2_gnn_in['w4_b'], 'L2_gnn_w5_w': _L2_gnn_in['w5_w'], 'L2_gnn_w5_b': _L2_gnn_in['w5_b'], 'L2_gnn_u5_w': _L2_gnn_in['u5_w'], 'L2_gnn_u5_b': _L2_gnn_in['u5_b'], 'L3_gnn_Wq': _L3_gnn_in['Wq'], 'L3_gnn_bq': _L3_gnn_in['bq'], 'L3_gnn_Wk': _L3_gnn_in['Wk'], 'L3_gnn_bk': _L3_gnn_in['bk'], 'L3_gnn_Wv': _L3_gnn_in['Wv'], 'L3_gnn_bv': _L3_gnn_in['bv'], 'L3_gnn_Wo': _L3_gnn_in['Wo'], 'L3_gnn_bo': _L3_gnn_in['bo']}

def reference(x, adj, L0_gnn_Wq, L0_gnn_Wk, L0_gnn_Wv, L1_gnn_weight, L1_gnn_bias, L2_gnn_w3_w, L2_gnn_w3_b, L2_gnn_u3_w, L2_gnn_u3_b, L2_gnn_w4_w, L2_gnn_w4_b, L2_gnn_w5_w, L2_gnn_w5_b, L2_gnn_u5_w, L2_gnn_u5_b, L3_gnn_Wq, L3_gnn_bq, L3_gnn_Wk, L3_gnn_bk, L3_gnn_Wv, L3_gnn_bv, L3_gnn_Wo, L3_gnn_bo):
    import jax
    import jax.numpy as jnp

    def _L0_gnn_ref(neuron_states, adjacency, Wq, Wk, Wv):
        import jax, jax.numpy as jnp
        import numpy as np
        B, N, D = (8, 1024, 256)
        q = jnp.einsum('bnd,ed->bne', neuron_states, Wq)
        k = jnp.einsum('bnd,ed->bne', neuron_states, Wk)
        v = jnp.einsum('bnd,ed->bne', neuron_states, Wv)
        rel = jnp.einsum('bnd,bmd->bnm', q, k)
        rel = adjacency.T[None, :, :] * rel
        rel = rel / jnp.linalg.norm(rel, axis=2, keepdims=True)
        return jnp.einsum('bnm,bmd->bnd', rel, v)

    def _L1_gnn_ref(x, adj, weight, bias):
        import jax, jax.numpy as jnp
        import numpy as np
        B, N, F_IN, F_OUT = (16, 1024, 256, 256)
        deg = adj.sum(axis=1)
        deg_inv_sqrt = jnp.where(deg > 0, jax.lax.rsqrt(deg), 0.0)
        norm_adj = adj * deg_inv_sqrt[:, None] * deg_inv_sqrt[None, :]
        support = jnp.einsum('bni,io->bno', x, weight)
        output = jnp.einsum('nm,bmo->bno', norm_adj, support)
        return output + bias

    def _L2_gnn_ref(x, in_mat, out_mat, w3_w, w3_b, u3_w, u3_b, w4_w, w4_b, w5_w, w5_b, u5_w, u5_b):
        import jax, jax.numpy as jnp
        import numpy as np
        B, N, D, T = (64, 128, 256, 3)

        def _lin(v, W, b):
            return jnp.einsum('...i,oi->...o', v, W) + b
        h = x
        for _ in range(T):
            a_in = jnp.einsum('nm,bmd->bnd', in_mat, h)
            a_out = jnp.einsum('nm,bmd->bnd', out_mat, h)
            av = jnp.concatenate([a_in, a_out], axis=-1)
            z = jax.nn.sigmoid(_lin(av, w3_w, w3_b) + _lin(h, u3_w, u3_b))
            r = jax.nn.sigmoid(_lin(av, w4_w, w4_b) + _lin(h, u3_w, u3_b))
            hv = jnp.tanh(_lin(av, w5_w, w5_b) + _lin(r * h, u5_w, u5_b))
            h = (1.0 - z) * h + z * hv
        return h

    def _L3_gnn_ref(x, adj, Wq, bq, Wk, bk, Wv, bv, Wo, bo):
        import jax, jax.numpy as jnp
        import numpy as np
        B, N, D, H = (4, 1024, 256, 8)
        HD = D // H
        b, n, d = x.shape
        q = (x @ Wq + bq).reshape(b, n, H, HD)
        k = (x @ Wk + bk).reshape(b, n, H, HD)
        v = (x @ Wv + bv).reshape(b, n, H, HD)
        scores = jnp.einsum('bqhd,bkhd->bhqk', q, k) / jnp.sqrt(jnp.float32(HD))
        scores = scores + (1.0 - adj)[None, None, :, :] * -1000000000.0
        attn = jax.nn.softmax(scores, axis=-1)
        out = jnp.einsum('bhqk,bkhd->bqhd', attn, v).reshape(b, n, d)
        return out @ Wo + bo
    x = _layernorm(x + _L0_gnn_ref(x, adj, L0_gnn_Wq, L0_gnn_Wk, L0_gnn_Wv), axis=-1)
    x = _layernorm(x + _L1_gnn_ref(x, adj, L1_gnn_weight, L1_gnn_bias), axis=-1)
    x = _layernorm(x + _L2_gnn_ref(x, adj, adj, L2_gnn_w3_w, L2_gnn_w3_b, L2_gnn_u3_w, L2_gnn_u3_b, L2_gnn_w4_w, L2_gnn_w4_b, L2_gnn_w5_w, L2_gnn_w5_b, L2_gnn_u5_w, L2_gnn_u5_b), axis=-1)
    x = _layernorm(x + _L3_gnn_ref(x, adj, L3_gnn_Wq, L3_gnn_bq, L3_gnn_Wk, L3_gnn_bk, L3_gnn_Wv, L3_gnn_bv, L3_gnn_Wo, L3_gnn_bo), axis=-1)
    return x

_drawn_inputs = setup_inputs


def setup_inputs(seed=0):
    import zlib

    import numpy as np

    out = dict(_drawn_inputs(seed))
    spreads = {'L1_gnn_bias': (0.0, 0.1),
     'L2_gnn_w3_b': (0.0, 0.1),
     'L2_gnn_u3_b': (0.0, 0.267),
     'L2_gnn_w4_b': (0.0, 2.0),
     'L2_gnn_w5_b': (0.0, 0.1),
     'L2_gnn_u5_b': (0.0, 0.1),
     'L3_gnn_bq': (0.0, 0.279),
     'L3_gnn_bk': (0.0, 2.0),
     'L3_gnn_bv': (0.0, 0.1),
     'L3_gnn_bo': (0.0, 0.1)}
    factors = {}
    for name, (base, spread) in spreads.items():
        noise = np.random.default_rng([zlib.crc32(name.encode()), seed]).standard_normal(out[name].shape)
        drawn = base * np.exp(spread * noise) if base else spread * noise
        out[name] = jnp.asarray(drawn.astype(out[name].dtype))
    for name, factor in factors.items():
        out[name] = (out[name] * factor).astype(out[name].dtype)
    return out
```

```python
import numpy as np
from contextlib import ExitStack

import concourse.bass as bass
from concourse import mybir

F32 = mybir.dt.float32
F32R = mybir.dt.float32r
ALU = mybir.AluOpType
ACT = mybir.ActivationFunctionType
AX = mybir.AxisListType

P = 128
LANES = 2
STEPS = 3
HEADS = 8
EPS = 1e-5
NEG = 1.0e9


def gnn_stack(nc, x, adj, wq0, wk0, wv0, w1, b1, w3, bw3, u3, bu3, w4, bw4, w5, bw5, u5, bu5,
              wq, bq, wk, bk, wv, bv, wo, bo, out):
    B, N, D = x.shape
    NT = N // P
    DT = D // P
    ITERS = B // LANES
    HD = D // HEADS
    PAIRS = HEADS // 2
    HEADJOBS = LANES * HEADS
    QT = NT * HEADJOBS
    UNIT = 2 * DT * N
    assert NT * D == DT * N and HD == 32 and N == 512 and D == 256

    xv = x.rearrange("(i l) (t p) d -> l i p t d", l=LANES, p=P)
    ov = out.rearrange("(i l) (t p) d -> l i p t d", l=LANES, p=P)

    with ExitStack() as ctx:
        def sb(name, shape, dt=F32):
            return ctx.enter_context(nc.sbuf_tensor(name, shape, dt))

        def sem(name):
            return ctx.enter_context(nc.semaphore(name))

        def sems(name, n=LANES):
            return [sem(f"{name}{k}") for k in range(n)]

        adj_n = sb("adj_n", [P, NT, N])
        mask = sb("mask", [P, NT, N])
        adjT = sb("adjT", [P, 2, NT, N], F32R)
        wnames = ["g0", "wv0", "w1", "w4", "wd", "w5", "u3", "u5", "wq", "wk", "wv"]
        W = {n: sb(f"W_{n}", [P, 2, DT, D], F32R) for n in wnames}
        Wo = sb("W_o", [P, 2, PAIRS, D], F32R)
        ident = sb("ident", [P, P])
        ones1 = sb("ones1", [P, 1])
        b1row = sb("b1row", [P, D])
        crow = sb("crow", [P, D])
        cols = sb("cols", [P, 10, DT])
        BW3, BU3, BW4, BW5, BU5, BQ, BK, BZ, BR, BH = range(10)
        bv4 = sb("bv4", [P, PAIRS])
        dinv = sb("dinv", [P, NT])
        dtmp = sb("dtmp", [P, 3, NT])
        mhalf = sb("mhalf", [P, 8])

        xn = sb("xn", [P, LANES, NT, D])
        stats = sb("stats", [P, LANES, NT, 6])
        mv = sb("mv", [P, LANES, NT, 2])
        veps = sb("veps", [P, LANES, NT])
        rstd = sb("rstd", [P, LANES, NT])
        rsd = sb("rsd", [P, LANES, NT])
        ssq = sb("ssq", [P, LANES, NT])
        rnorm = sb("rnorm", [P, LANES, NT])
        nmax = sb("nmax", [P, 8])
        esum = sb("esum", [P, 8])
        rsum = sb("rsum", [P, 8])
        fa = sb("fa", [P, 5 * DT * N])
        ra = sb("ra", [P, 11 * UNIT], F32R)

        def fview(word, a, b):
            return fa[:, word:word + a * b].rearrange("p (a b) -> p a b", a=a)

        def rview(unit, a, b, units=1):
            return ra[:, unit * UNIT:(unit + units) * UNIT].rearrange("p (s a b) -> p s a b", a=a, b=b)

        def f32(v):
            return v.bitcast(F32)

        H, L = 0, 1
        XNS = [rview(0, NT, D), rview(1, NT, D)]
        HTS = [rview(2, DT, N), rview(3, DT, N)]
        AB = [rview(4, DT, N), rview(5, DT, N)]
        RELH = [ra[:, (2 + l) * UNIT:(3 + l) * UNIT].rearrange("p (a b) -> p a b", a=NT) for l in range(2)]
        RELL = [ra[:, (4 + l) * UNIT:(5 + l) * UNIT].rearrange("p (a b) -> p a b", a=NT) for l in range(2)]
        STK = rview(0, 2, N, units=2)
        SRC = [rview(2, 4, N, units=2), rview(4, 4, N, units=2)]
        VP = ra[:, 6 * UNIT:8 * UNIT].rearrange("p (a e c) -> p a e c", e=2, c=P)
        X3T = rview(8, DT, N)
        PT = rview(9, 2, N, units=2)
        REL = [fview(0, NT, N), fview(NT * N, NT, N)]
        XS = [fview(0, NT, D), fview(NT * N, NT, D)]
        hT = [fview(0, DT, N), fview(DT * N, DT, N)]
        tr, tz, thv = [fview((2 + k) * DT * N, DT, N) for k in range(3)]
        SC = fview(0, 8, N)

        ps = ctx.enter_context(nc.psum_tensor("ps", [P, 8, N], F32))

        def pair(b):
            return ps[:, b:b + 2, :]

        def natural(b):
            return ps[:, b:b + 2, :].rearrange("p b (t d) -> p (b t) d", d=D)

        q_w = sem("setup_loads"); q_adj = sem("setup_adj_load"); q_prep = sem("setup_dve")
        q_act = sem("setup_act"); q_pe = sem("setup_pe"); q_pool = sem("setup_pool")
        c_dve = sem("dve_chain"); c_dve2 = sem("dve_chain_l2"); c_pool = sem("pool_chain")
        x_in = sems("x_loaded"); out_done = sems("out_stored")
        xT_ps = sems("xT_ps"); xT_h = sems("xT_h"); xT_l = sems("xT_l")
        xs_l = sems("x_split")
        y_ps = sems("y_ps"); y_h = sems("y_h"); y_l = sems("y_l")
        s_ps = sems("gram_ps"); rel_f = sems("rel_masked"); rel_h = sems("rel_h"); rel_l = sems("rel_l")
        sq_f = sems("rel_squared"); sq_s = sems("squares_summed"); ssq_ps = sems("ssq_ps")
        ssq_c = sems("ssq_copied"); rn_r = sems("rnorm_ready")
        u_ps = sems("u_ps"); u_h = sems("u_h"); u_l = sems("u_l"); o_ps = sems("o_ps")
        ln_v = sems("ln_var"); ln_r = sems("ln_rstd")
        x1s_f = sems("x1_scaled"); x1s_h = sems("x1s_h"); x1s_l = sems("x1s_l"); xb_r = sems("x1_plus_bias")
        t_ps = sems("t_ps"); t_h = sems("t_h"); t_l = sems("t_l"); o1_ps = sems("o1_ps")
        x2_r = sems("x2_ready"); x2_h = sems("x2_h")
        hT_ps = sems("hT_ps"); hT_h = sems("hT_h")
        h_f = sems("h_ready"); hT_l = sems("hT_l")
        xn_h = sems("hn_h"); xn_l = sems("hn_l")
        tp_ps = sems("hn_ps")
        a_ps = sem("a_ps"); a_h = sem("a_h"); a_l = sem("a_l")
        r_ps = sem("r_ps"); r_t = sem("r_tanh"); z_ps = sem("z_ps"); z_t = sem("z_tanh")
        v_ps = sem("hv_ps"); v_t = sem("hv_tanh"); rh_l = sem("rh_l")
        x3_r = sems("x3_ready"); x3_ps = sems("x3T_ps"); x3_h = sems("x3T_h"); x3_l = sems("x3T_l")
        q_ps = sems("q_ps"); k_ps = sems("k_ps"); vv_ps = sems("v_ps")
        q_h = sems("q_h"); k_h = sems("k_h"); vv_h = sems("v_h")
        q_l = sems("q_l"); k_l = sems("k_l"); vv_l = sems("v_l")
        stk = sems("stacked", 4)
        sc_ps = sem("score_ps"); ttr = sem("score_masked"); ex = sem("score_exp"); nrm = sem("prob_ready")
        rs_r = sem("row_sum_inverted")
        pt_ps = sem("probT_ps"); pt_h = sem("probT_h"); pt_l = sem("probT_l"); pv = sem("pv_done")
        ot_h = sem("ot_h"); ot_l = sem("ot_l")
        yo_ps = sems("attn_out_ps"); yo_r = sems("attn_out_read"); xc_r = sems("x3_plus_const")
        x4_r = sems("x4_ready")

        CHAIN, CHAIN2, PCHAIN = 28, 8, 2
        Q_PREP_ALL, Q_PE_ALL = 40, 12

        gates = {"dve": sem("dve_gate"), "pool": sem("pool_gate"), "sp": sem("sp_gate")}

        def settle(eng, who):
            eng.sem_inc(gates[who], 1)

        block = ctx.enter_context(nc.Block())

        st3, st4, st5 = [fview(k * DT * 2 * D, DT, 2 * D) for k in range(3)]
        stu3, stu5, stv0, stk0 = [fview(3 * DT * 2 * D + k * DT * D, DT, D) for k in range(4)]
        stq0, st1 = [xn[:, 0, 2 * k:2 * k + 2, :] for k in range(2)]
        sto = xn[:, 1, :, :]
        stq, stkk, stvv = [mask[:, k, :].rearrange("p (a b) -> p a b", a=DT) for k in range(3)]
        bvb = mask[:, 3, :].rearrange("p (a b) -> p a b", a=PAIRS)

        @block.sync
        def _(sp):
            def rows(ap):
                return ap.rearrange("(t p) d -> p t d", p=P)

            sp.dma_start(adj_n[:, :, :], rows(adj)).then_inc(q_adj, 16)
            for dst, src in ((st3, w3), (st4, w4), (st5, w5), (stu3, u3), (stu5, u5), (stv0, wv0),
                             (stk0, wk0), (stq0, wq0), (st1, w1), (stq, wq), (stkk, wk), (stvv, wv)):
                sp.dma_start(dst, rows(src)).then_inc(q_w, 16)
            wo_rows = wo.rearrange("(j e p) d -> e p j d", e=2, p=HD)
            bv_rows = bv.rearrange("(j e p) -> e p j", e=2, p=HD)
            for e in range(2):
                for c in range(2):
                    part = (2 * e + c) * HD
                    sp.dma_start(sto[part:part + HD, :, :], wo_rows[e]).then_inc(q_w, 16)
                    with nc.allow_non_contiguous_dma("a few words of bias"):
                        sp.dma_start(bv4[part:part + HD, :], bv_rows[e]).then_inc(q_w, 16)
            with nc.allow_non_contiguous_dma("a few words of bias"):
                for k, src in ((BW3, bw3), (BU3, bu3), (BW4, bw4), (BW5, bw5), (BU5, bu5), (BQ, bq), (BK, bk)):
                    sp.dma_start(cols[:, k, :], src.rearrange("(t p) -> p t", p=P)).then_inc(q_w, 16)
            sp.dma_start(b1row[:, :], b1.rearrange("(a d) -> a d", a=1).broadcast_to((P, D))).then_inc(q_w, 16)
            sp.dma_start(crow[:, :], bo.rearrange("(a d) -> a d", a=1).broadcast_to((P, D))).then_inc(q_w, 16)
            sp.wait_ge(q_prep, Q_PREP_ALL)
            sp.wait_ge(q_pe, Q_PE_ALL)
            for l in range(LANES):
                sp.sem_inc(out_done[l], 16)

            with sp.Fori(0, ITERS) as it:
                for n in range(HEADJOBS):
                    l, h, slot = n // HEADS, n % HEADS, n % 4
                    if h == 0:
                        sp.wait_ge(q_l[l], it + 1)
                        sp.wait_ge(k_l[l], it + 1)
                        settle(sp, "sp")
                    if n == 0:
                        for m in range(LANES):
                            sp.wait_ge(x3_r[m], it + 1)
                        settle(sp, "sp")
                    if n >= 4:
                        sp.wait_ge(sc_ps, it * QT + (n - 3) * NT)
                    g, r = h // 4, (h % 4) * HD
                    for k, parts in ((0, (0, 0, 1, 1)), (1, (2, 3, 2, 3))):
                        for c, part in enumerate(parts):
                            sp.dma_start(f32(STK[c * HD:(c + 1) * HD, slot, k, :]),
                                         f32(SRC[l][r:r + HD, g, part, :])).then_inc(stk[slot], 16)
                    if n == HEADS + 6:
                        sp.wait_ge(x4_r[0], it + 1)
                        settle(sp, "sp")
                        sp.dma_start(ov[0][it], xn[:, 0, :, :]).then_inc(out_done[0], 16)
                sp.wait_ge(x4_r[1], it + 1)
                settle(sp, "sp")
                sp.dma_start(ov[1][it], xn[:, 1, :, :]).then_inc(out_done[1], 16)
            for l in range(LANES):
                sp.wait_ge(out_done[l], 16 * (ITERS + 1))

        @block.gpsimd
        def _(gp):
            nc.gpsimd.memset(ident[:, :], 0.0).then_inc(q_pool, 1)
            nc.gpsimd.memset(mhalf[:, 0:4], -0.5).then_inc(q_pool, 1)
            nc.gpsimd.memset(mhalf[:, 4:8], -1.0).then_inc(q_pool, 1)
            nc.gpsimd.memset(ones1[:, :], 1.0).then_inc(q_pool, 1)
            gp.wait_ge(q_pool, 4)
            nc.gpsimd.affine_select(out=ident[:, :], in_=ident[:, :], compare_op=ALU.not_equal, fill=1.0,
                                    base=0, pattern=[[-1, P]], channel_multiplier=1).then_inc(q_pool, 1)
            gp.wait_ge(q_prep, 2)
            nc.gpsimd.tensor_tensor(dtmp[:, 2, :], dtmp[:, 1, :], mhalf[:, 0:NT], ALU.pow).then_inc(q_pool, 1)

            with gp.Fori(0, ITERS) as it:
                done = [0]

                def link(ins):
                    done[0] += 1
                    ins.then_inc(c_pool, 1)
                    gp.wait_ge(c_pool, it * PCHAIN + done[0])

                def rstd_of(l, k):
                    gp.wait_ge(ln_v[l], it * 4 + (k + 1))
                    nc.gpsimd.tensor_tensor(rstd[:, l, :], veps[:, l, :], mhalf[:, 0:NT],
                                            ALU.pow).then_inc(ln_r[l], 1)

                for l in range(LANES):
                    gp.wait_ge(out_done[l], it * 16 + 16)
                    settle(gp, "pool")
                    gp.dma_start(xn[:, l, :, :], xv[l][it]).then_inc(x_in[l], 16)
                    gp.wait_ge(x_in[l], it * 16 + 16)
                    settle(gp, "pool")
                    link(nc.gpsimd.tensor_scalar(XNS[l][:, H], xn[:, l], 1.0, 1.0, ALU.mult, ALU.mult))
                    nc.gpsimd.tensor_tensor(XNS[l][:, L], xn[:, l], f32(XNS[l][:, H]),
                                            ALU.subtract).then_inc(xs_l[l], 1)
                for l in range(LANES):
                    gp.wait_ge(sq_f[l], it + 1)
                    for t in range(1, NT):
                        ins = nc.gpsimd.tensor_tensor(REL[l][:, 0], REL[l][:, 0], REL[l][:, t], ALU.add)
                        if t < NT - 1:
                            ins.then_inc(sq_s[l], 1)
                            gp.wait_ge(sq_s[l], it * (NT - 1) + t)
                        else:
                            ins.then_inc(sq_s[l], 1)
                for l in range(LANES):
                    gp.wait_ge(ssq_c[l], it + 1)
                    nc.gpsimd.tensor_tensor(rnorm[:, l, :], ssq[:, l, :], mhalf[:, 0:NT],
                                            ALU.pow).then_inc(rn_r[l], 1)
                    rstd_of(l, 0)
                for l in range(LANES):
                    gp.wait_ge(x1s_f[l], it + 1)
                    for t in range(NT):
                        ins = nc.gpsimd.tensor_tensor(xn[:, l, t], xn[:, l, t], b1row[:, :], ALU.add)
                    ins.then_inc(xb_r[l], 1)
                for l in range(LANES):
                    rstd_of(l, 1)
                for l in range(LANES):
                    rstd_of(l, 2)
                for l in range(LANES):
                    gp.wait_ge(x3_ps[l], it + 1)
                    for t in range(NT):
                        ins = nc.gpsimd.tensor_tensor(xn[:, l, t], xn[:, l, t], crow[:, :], ALU.add)
                    ins.then_inc(xc_r[l], 1)
                for n in range(HEADJOBS):
                    gp.wait_ge(ex, it * QT + (n + 1) * NT)
                    s0 = (n % 2) * NT
                    nc.gpsimd.tensor_tensor(rsum[:, s0:s0 + NT], esum[:, s0:s0 + NT], mhalf[:, 4:4 + NT],
                                                  ALU.pow).then_inc(rs_r, 1)
                    gp.wait_ge(rs_r, it * HEADJOBS + (n + 1))
                    settle(gp, "pool")
                    for t in range(NT):
                        nc.gpsimd.tensor_scalar(SC[:, s0 + t], SC[:, s0 + t], rsum[:, s0 + t:s0 + t + 1], 1.0,
                                                ALU.mult, ALU.mult).then_inc(nrm, 1)
                    if n == HEADS + 2:
                        rstd_of(0, 3)
                rstd_of(1, 3)
                assert done[0] == PCHAIN

        @block.scalar
        def _(act):
            def copy(dst, src):
                return nc.scalar.copy(dst, src)

            act.wait_ge(q_prep, 12)
            copy(W["w1"][:, H], st1).then_inc(q_act, 1)
            copy(W["wq"][:, H], stq).then_inc(q_act, 1)
            copy(W["wk"][:, H], stkk).then_inc(q_act, 1)
            copy(W["wv"][:, H], stvv).then_inc(q_act, 1)
            copy(Wo[:, H], sto).then_inc(q_act, 1)
            for k, name in enumerate(["wv0", "w4", "wd", "w5", "u3", "u5", "g0"]):
                act.wait_ge(q_pe, k + 1)
                copy(W[name][:, H], ps[:, k, :].rearrange("p (a b) -> p a b", a=DT)).then_inc(q_act, 1)
            for t in range(NT):
                act.wait_ge(q_pe, 9 + t)
                copy(adjT[:, H, t], ps[:, t, :]).then_inc(q_act, 1)

            act.sem_inc(z_t, 1)
            act.sem_inc(v_t, 1)

            with act.Fori(0, ITERS) as it:
                v = it + 1

                for l in range(LANES):
                    act.wait_ge(xT_ps[l], v)
                    copy(HTS[l][:, H], pair(4 * l)).then_inc(xT_h[l], 1)
                for l in range(LANES):
                    act.wait_ge(y_ps[l], v)
                    copy(AB[l][:, H], pair(4 * l + 2)).then_inc(y_h[l], 1)
                for l in range(LANES):
                    for c in range(2):
                        act.wait_ge(rel_f[l], it * 2 + (c + 1))
                        copy(RELH[l][:, 2 * c:2 * c + 2], REL[l][:, 2 * c:2 * c + 2]).then_inc(rel_h[l], 1)
                for l in range(LANES):
                    act.wait_ge(rel_l[l], v)
                    nc.scalar.activation(REL[l][:, :, :], REL[l][:, :, :], ACT.Square).then_inc(sq_f[l], 1)
                for l in range(LANES):
                    act.wait_ge(u_ps[l], v)
                    copy(AB[l][:, H], pair(4 * l)).then_inc(u_h[l], 1)
                for l in range(LANES):
                    act.wait_ge(x1s_f[l], v)
                    copy(XNS[l][:, H], XS[l]).then_inc(x1s_h[l], 1)
                for l in range(LANES):
                    act.wait_ge(t_ps[l], v)
                    copy(AB[l][:, H], pair(4 * l)).then_inc(t_h[l], 1)
                for l in range(LANES):
                    if l == 0:
                        act.wait_ge(x2_r[0], v)
                        copy(XNS[0][:, H], xn[:, 0]).then_inc(xn_h[0], 1)
                    act.wait_ge(hT_ps[l], v)
                    copy(HTS[l][:, H], pair(4 * l)).then_inc(hT_h[l], 1)
                with act.Fori(0, STEPS) as j:
                    for l in range(LANES):
                        m = it * 6 + j * 2 + (l + 1)
                        o = 1 - l
                        act.wait_ge(a_ps, m)
                        copy(AB[0][:, H], pair(0)).then_inc(a_h, 1)
                        act.wait_ge(r_ps, m)
                        for d in range(DT):
                            ins = nc.scalar.activation(tr[:, d], ps[:, 2 + d], ACT.Tanh,
                                                       bias=cols[:, BR, d:d + 1], scale=0.5)
                        ins.then_inc(r_t, 1)
                        act.wait_ge(tp_ps[o], it * (3 + o) + j + 1)
                        copy(XNS[o][:, H], natural(6)).then_inc(xn_h[o], 1)
                        act.wait_ge(z_ps, m)
                        for d in range(DT):
                            ins = nc.scalar.activation(tz[:, d], ps[:, 2 + d], ACT.Tanh,
                                                       bias=cols[:, BZ, d:d + 1], scale=0.5)
                        ins.then_inc(z_t, 1)
                        act.wait_ge(v_ps, m)
                        for d in range(DT):
                            ins = nc.scalar.activation(thv[:, d], ps[:, 4 + d], ACT.Tanh,
                                                       bias=cols[:, BH, d:d + 1])
                        ins.then_inc(v_t, 1)
                        act.wait_ge(h_f[l], it * 4 + j + 2)
                        copy(HTS[l][:, H], hT[l]).then_inc(hT_h[l], 1)
                act.wait_ge(tp_ps[1], it * 4 + 4)
                copy(XNS[1][:, H], natural(6)).then_inc(xn_h[1], 1)
                def proj_hi(sem_ps, sem_h, l, b, k, bias):
                    act.wait_ge(sem_ps[l], v)
                    for d in range(DT):
                        ins = nc.scalar.activation(SRC[l][:, d, 2 * k], ps[:, b + d], ACT.Identity,
                                                   bias=cols[:, bias, d:d + 1])
                    ins.then_inc(sem_h[l], 1)

                def v_hi(l, b):
                    act.wait_ge(vv_ps[l], v)
                    src = natural(b).rearrange("p t (j e c) -> p (t j) e c", e=2, c=HD)
                    copy(VP[:, :, 0, 0:HD], src[:, :, 0])
                    copy(VP[:, :, 1, 2 * HD:3 * HD], src[:, :, 1]).then_inc(vv_h[l], 1)

                for l in range(LANES):
                    act.wait_ge(x3_ps[l], v)
                    if l == 1:
                        act.wait_ge(vv_ps[0], v)
                    copy(X3T[:, H], pair(4)).then_inc(x3_h[l], 1)
                    proj_hi(q_ps, q_h, l, 0, 0, BQ)
                    proj_hi(k_ps, k_h, l, 2, 1, BK)
                    if l == 0:
                        v_hi(0, 6)
                for n in range(-2, HEADJOBS + 1):
                    for q in range(NT):
                        if n + 2 < HEADJOBS:
                            g = 4 * ((n + 2) % 2) + q
                            act.wait_ge(ttr, it * QT + ((n + 2) * NT + q + 1 + 2))
                            nc.scalar.activation(SC[:, g], SC[:, g], ACT.Exp, bias=nmax[:, g:g + 1], scale=-1.0,
                                                 accum_out=esum[:, g:g + 1]).then_inc(ex, 1)
                        if 0 <= n < HEADJOBS:
                            act.wait_ge(pt_ps, it * QT + (n * NT + q + 1))
                            if n > 0:
                                act.wait_ge(pv, it * QT + ((n - 1) * NT + q + 1))
                            copy(PT[:, q, H], ps[:, 4 + q]).then_inc(pt_h, 1)
                    if n >= 2 and n % 2 == 0:
                        pr = n // 2 - 1
                        act.wait_ge(pv, it * QT + n * NT)
                        copy(SRC[pr // PAIRS][:, (pr % PAIRS) // 2, 2 * (pr % 2) + H], ps[:, 2 + pr % 2]
                             ).then_inc(ot_h, 1)
                    if n == HEADS:
                        v_hi(1, 0)

        @block.vector
        def _(dve):
            TT, STT, TS = nc.vector.tensor_tensor, nc.vector.scalar_tensor_tensor, nc.vector.tensor_scalar
            steps = [0]

            def prep(ins):
                steps[0] += 1
                ins.then_inc(q_prep, 1)
                dve.wait_ge(q_prep, steps[0])

            dve.wait_ge(q_adj, 16)
            prep(nc.vector.reduce_sum(dtmp[:, 0, :], adj_n[:, :, :], AX.X))
            prep(TS(dtmp[:, 1, :], dtmp[:, 0, :], 1.2e-38, None, ALU.max))
            dve.wait_ge(q_w, 16 * (12 + 8 + 7 + 2))
            prep(TT(st3[:, :, 0:D], st3[:, :, 0:D], st3[:, :, D:2 * D], ALU.add))
            prep(TT(st4[:, :, 0:D], st4[:, :, 0:D], st4[:, :, D:2 * D], ALU.add))
            prep(TT(st5[:, :, 0:D], st5[:, :, 0:D], st5[:, :, D:2 * D], ALU.add))
            prep(TT(st3[:, :, 0:D], st3[:, :, 0:D], st4[:, :, 0:D], ALU.subtract))
            prep(TS(stu5, stu5, 0.5, None, ALU.mult))
            prep(TS(stq, stq, float(HD) ** -0.5, None, ALU.mult))
            prep(TS(cols[:, BQ, :], cols[:, BQ, :], float(HD) ** -0.5, None, ALU.mult))
            prep(TT(cols[:, BZ, :], cols[:, BW3, :], cols[:, BU3, :], ALU.add))
            prep(TT(cols[:, BR, :], cols[:, BW4, :], cols[:, BU3, :], ALU.add))
            prep(TT(cols[:, BH, :], cols[:, BW5, :], cols[:, BU5, :], ALU.add))
            prep(TS(cols[:, BZ, :], cols[:, BZ, :], 0.5, None, ALU.mult))
            prep(TS(cols[:, BR, :], cols[:, BR, :], 0.5, None, ALU.mult))
            dve.wait_ge(q_pool, 5)
            for j in range(PAIRS):
                prep(TS(bvb[:, j, :], ident[:, :], 0.0, bv4[:, j:j + 1], ALU.mult, ALU.add))
            prep(TS(bvb[:, :, :], bvb[:, :, :], 0.5, None, ALU.mult))
            dve.wait_ge(q_pool, 6)
            prep(TS(dtmp[:, 0, :], dtmp[:, 0, :], 0.0, None, ALU.is_gt))
            prep(TT(dinv[:, :], dtmp[:, 0, :], dtmp[:, 2, :], ALU.mult))
            n_act = 0
            for dst, src in (("w1", st1), ("wq", stq), ("wk", stkk), ("wv", stvv)):
                n_act += 1
                dve.wait_ge(q_act, n_act)
                prep(TT(W[dst][:, L], src, f32(W[dst][:, H]), ALU.subtract))
            n_act += 1
            dve.wait_ge(q_act, n_act)
            prep(TT(Wo[:, L], sto, f32(Wo[:, H]), ALU.subtract))
            for k, name in enumerate(["wv0", "w4", "wd", "w5", "u3", "u5", "g0"]):
                n_act += 1
                dve.wait_ge(q_act, n_act)
                prep(TT(W[name][:, L], ps[:, k, :].rearrange("p (a b) -> p a b", a=DT), f32(W[name][:, H]),
                        ALU.subtract))
            dve.wait_ge(q_pe, 8)
            prep(TT(crow[:, :], crow[:, :], ps[:, 7, 0:D], ALU.add))
            for t in range(NT):
                n_act += 1
                dve.wait_ge(q_act, n_act)
                prep(TT(adjT[:, L, t], ps[:, t, :], f32(adjT[:, H, t]), ALU.subtract))
            prep(TS(mask[:, :, :], adj_n[:, :, :], 1.0, NEG, ALU.subtract, ALU.mult))
            prep(nc.vector.memset(f32(ra[:, 6 * UNIT:8 * UNIT]), 0.0))
            assert steps[0] == Q_PREP_ALL

            for _ in range(2):
                dve.sem_inc(ttr, 1)

            with dve.Fori(0, ITERS) as it:
                v = it + 1
                done = [0]

                def link(ins):
                    done[0] += 1
                    ins.then_inc(c_dve, 1)
                    dve.wait_ge(c_dve, it * CHAIN + done[0])

                def lo(dst, src, hi, wait_sem, value, signal):
                    dve.wait_ge(wait_sem, value)
                    TT(dst, src, f32(hi), ALU.subtract).then_inc(signal, 1)

                def layer_norm(l, k, signal, scaled=False):
                    for t in range(NT):
                        ins = nc.vector.bn_stats(stats[:, l, t, :], xn[:, l, t, :])
                    link(ins)
                    settle(dve, "dve")
                    for t in range(NT):
                        ins = nc.vector.bn_aggr(mv[:, l, t, :], stats[:, l, t, :])
                    link(ins)
                    TS(veps[:, l, :], mv[:, l, :, 1], EPS, None, ALU.add).then_inc(ln_v[l], 1)
                    dve.wait_ge(ln_r[l], it * 4 + (k + 1))
                    if scaled:
                        link(TT(rsd[:, l, :], rstd[:, l, :], dinv[:, :], ALU.mult))
                        for t in range(NT):
                            ins = TS(XS[l][:, t], xn[:, l, t], mv[:, l, t, 0:1], rsd[:, l, t:t + 1],
                                     ALU.subtract, ALU.mult)
                        link(ins)
                    for t in range(NT):
                        ins = TS(xn[:, l, t], xn[:, l, t], mv[:, l, t, 0:1], rstd[:, l, t:t + 1],
                                 ALU.subtract, ALU.mult)
                    ins.then_inc(signal, 1)

                for l in range(LANES):
                    lo(HTS[l][:, L], pair(4 * l), HTS[l][:, H], xT_h[l], v, xT_l[l])
                for l in range(LANES):
                    lo(AB[l][:, L], pair(4 * l + 2), AB[l][:, H], y_h[l], v, y_l[l])
                for l in range(LANES):
                    dve.wait_ge(s_ps[l], v)
                    for c in range(2):
                        t = slice(2 * c, 2 * c + 2)
                        TT(REL[l][:, t], pair(4 * l + 2 * c), adj_n[:, t], ALU.mult).then_inc(rel_f[l], 1)
                    for c in range(2):
                        t = slice(2 * c, 2 * c + 2)
                        dve.wait_ge(rel_h[l], it * 2 + (c + 1))
                        ins = TT(RELL[l][:, t], REL[l][:, t], f32(RELH[l][:, t]), ALU.subtract)
                    ins.then_inc(rel_l[l], 1)
                for l in range(LANES):
                    lo(AB[l][:, L], pair(4 * l), AB[l][:, H], u_h[l], v, u_l[l])
                for l in range(LANES):
                    dve.wait_ge(ssq_ps[l], v)
                    nc.vector.tensor_copy(ssq[:, l, :], ps[:, 4 * l, 0:NT]).then_inc(ssq_c[l], 1)
                    dve.wait_ge(rn_r[l], v)
                    dve.wait_ge(o_ps[l], v)
                    for t in range(NT):
                        ins = STT(xn[:, l, t], natural(4 * l + 2)[:, t], rnorm[:, l, t:t + 1], xn[:, l, t],
                                  ALU.mult, ALU.add)
                    link(ins)
                    layer_norm(l, 0, x1s_f[l], scaled=True)
                    lo(XNS[l][:, L], XS[l], XNS[l][:, H], x1s_h[l], v, x1s_l[l])
                for l in range(LANES):
                    lo(AB[l][:, L], pair(4 * l), AB[l][:, H], t_h[l], v, t_l[l])
                for l in range(LANES):
                    dve.wait_ge(o1_ps[l], v)
                    dve.wait_ge(xb_r[l], v)
                    for t in range(NT):
                        ins = STT(xn[:, l, t], natural(4 * l + 2)[:, t], dinv[:, t:t + 1], xn[:, l, t],
                                  ALU.mult, ALU.add)
                    link(ins)
                    layer_norm(l, 1, x2_r[l])
                    if l == 0:
                        lo(XNS[0][:, L], xn[:, 0], XNS[0][:, H], xn_h[0], it * 4 + 1, xn_l[0])
                for l in range(LANES):
                    dve.wait_ge(hT_h[l], it * 4 + 1)
                    nc.vector.tensor_copy(hT[l], pair(4 * l)).then_inc(h_f[l], 1)
                    TT(HTS[l][:, L], pair(4 * l), f32(HTS[l][:, H]), ALU.subtract).then_inc(hT_l[l], 1)
                with dve.Fori(0, STEPS) as j:
                    n2 = [0]

                    def link2(ins):
                        n2[0] += 1
                        ins.then_inc(c_dve2, 1)
                        dve.wait_ge(c_dve2, it * (STEPS * CHAIN2) + j * CHAIN2 + n2[0])

                    for l in range(LANES):
                        m = it * 6 + j * 2 + (l + 1)
                        o = 1 - l
                        lo(AB[0][:, L], pair(0), AB[0][:, H], a_h, m, a_l)
                        dve.wait_ge(r_t, m)
                        link2(STT(tr, tr, 1.0, hT[l], ALU.add, ALU.mult))
                        link2(nc.vector.tensor_copy(AB[1][:, H], tr))
                        TT(AB[1][:, L], tr, f32(AB[1][:, H]), ALU.subtract).then_inc(rh_l, 1)
                        lo(XNS[o][:, L], natural(6), XNS[o][:, H], xn_h[o], it * 4 + j + (1 if o == 1 else 2),
                           xn_l[o])
                        dve.wait_ge(v_t, m + 1)
                        link2(TT(thv, thv, hT[l], ALU.subtract))
                        dve.wait_ge(z_t, m + 1)
                        link2(STT(tz, tz, 1.0, thv, ALU.add, ALU.mult))
                        STT(hT[l], tz, 0.5, hT[l], ALU.mult, ALU.add).then_inc(h_f[l], 1)
                        lo(HTS[l][:, L], hT[l], HTS[l][:, H], hT_h[l], it * 4 + j + 2, hT_l[l])
                    assert n2[0] == CHAIN2, n2
                for l in range(LANES):
                    if l == 1:
                        lo(XNS[1][:, L], natural(6), XNS[1][:, H], xn_h[1], it * 4 + 4, xn_l[1])
                    dve.wait_ge(xn_l[l], it * 4 + 4)
                    hs = fview(l * DT * N, NT, D)
                    link(TT(hs, f32(XNS[l][:, H]), f32(XNS[l][:, L]), ALU.add))
                    link(TT(xn[:, l], xn[:, l], hs, ALU.add))
                    layer_norm(l, 2, x3_r[l])
                def proj_lo(sem_h, sem_l, l, b, k, bias):
                    dve.wait_ge(sem_h[l], v)
                    for d in range(DT):
                        ins = STT(SRC[l][:, d, 2 * k + L], ps[:, b + d], cols[:, bias, d:d + 1],
                                  f32(SRC[l][:, d, 2 * k]), ALU.add, ALU.subtract)
                    ins.then_inc(sem_l[l], 1)

                def v_lo(l, b):
                    dve.wait_ge(vv_h[l], v)
                    src = natural(b).rearrange("p t (j e c) -> p (t j) e c", e=2, c=HD)
                    TT(VP[:, :, 0, HD:2 * HD], src[:, :, 0], f32(VP[:, :, 0, 0:HD]), ALU.subtract)
                    TT(VP[:, :, 1, 3 * HD:4 * HD], src[:, :, 1], f32(VP[:, :, 1, 2 * HD:3 * HD]),
                       ALU.subtract).then_inc(vv_l[l], 1)

                def finish(l):
                    dve.wait_ge(yo_ps[l], v)
                    dve.wait_ge(xc_r[l], v)
                    ins = TT(xn[:, l], natural(2), xn[:, l], ALU.add)
                    ins.then_inc(yo_r[l], 1)
                    dve.wait_ge(yo_r[l], v)
                    layer_norm(l, 3, x4_r[l])

                for l in range(LANES):
                    lo(X3T[:, L], pair(4), X3T[:, H], x3_h[l], v, x3_l[l])
                    proj_lo(q_h, q_l, l, 0, 0, BQ)
                    proj_lo(k_h, k_l, l, 2, 1, BK)
                    if l == 0:
                        v_lo(0, 6)
                for n in range(-2, HEADJOBS + 1):
                    def masked(q):
                        if n + 2 < HEADJOBS:
                            g = 4 * ((n + 2) % 2) + q
                            dve.wait_ge(sc_ps, it * QT + ((n + 2) * NT + q + 1))
                            if n >= 0 and q == 0:
                                dve.wait_ge(pt_ps, it * QT + (n + 1) * NT)
                            settle(dve, "dve")
                            nc.vector.tensor_tensor_reduce(
                                out=SC[:, g], in0=ps[:, ((n + 2) * NT + q) % 2], in1=mask[:, q], scale=-1.0,
                                scalar=3.0e38, op0=ALU.add, op1=ALU.min, accum_out=nmax[:, g:g + 1]
                            ).then_inc(ttr, 1)

                    def prob_lo(q):
                        if 0 <= n < HEADJOBS:
                            lo(PT[:, q, L], ps[:, 4 + q], PT[:, q, H], pt_h, it * QT + (n * NT + q + 1), pt_l)

                    masked(0)
                    masked(1)
                    masked(2)
                    prob_lo(0)
                    masked(3)
                    prob_lo(1)
                    prob_lo(2)
                    prob_lo(3)
                    if n >= 2 and n % 2 == 0:
                        pr = n // 2 - 1
                        tile, k = (pr % PAIRS) // 2, 2 * (pr % 2)
                        lo(SRC[pr // PAIRS][:, tile, k + L], ps[:, 2 + pr % 2], SRC[pr // PAIRS][:, tile, k + H],
                           ot_h, it * (HEADJOBS // 2) + (pr + 1), ot_l)
                    if n == HEADS:
                        v_lo(1, 0)
                        finish(0)
                finish(1)
                assert done[0] == CHAIN, done

        @block.tensor
        def _(pe):
            mm = nc.tensor.matmul

            def mm3(dst, w_h, w_l, m_h, m_l, first, last, again=False):
                mm(dst, w_h, m_h, start=first, stop=False, skip_group_check=again)
                mm(dst, w_l, m_h, start=False, stop=False, skip_group_check=again)
                return mm(dst, w_h, m_l, start=False, stop=last, skip_group_check=again)

            def through(b, w, src, first=True, last=True, again=False):
                for o in range(DT):
                    c = slice(o * P, (o + 1) * P)
                    for d in range(DT):
                        ins = mm3(ps[:, b + o, :], w[:, H, d, c], w[:, L, d, c], src[:, H, d], src[:, L, d],
                                  first and d == 0, last and d == DT - 1, again)
                return ins

            def gather(b, xs, mh, ml):
                for o in range(DT):
                    c = slice(o * P, (o + 1) * P)
                    for t in range(NT):
                        ins = mm3(ps[:, b + o, :], xs[:, H, t, c], xs[:, L, t, c], mh[:, t], ml[:, t],
                                  t == 0, t == NT - 1)
                return ins

            def to_natural(b, src, w):
                dst = natural(b)
                for t in range(NT):
                    c = slice(t * P, (t + 1) * P)
                    for d in range(DT):
                        ins = mm3(dst[:, t], src[:, H, d, c], src[:, L, d, c], w[:, H, d], w[:, L, d],
                                  d == 0, d == DT - 1)
                return ins

            def transpose_nodes(b, src):
                for d in range(DT):
                    for t in range(NT):
                        ins = nc.tensor.transpose(ps[:, b + d, t * P:(t + 1) * P], src[:, t, d * P:(d + 1) * P],
                                                  ident[:, :])
                return ins

            def transpose_features(b, src):
                dst = natural(b)
                for t in range(NT):
                    for d in range(DT):
                        ins = nc.tensor.transpose(dst[:, t, d * P:(d + 1) * P], src[:, d, t * P:(t + 1) * P],
                                                  ident[:, :])
                return ins

            pe.wait_ge(q_prep, 19)
            pe.wait_ge(q_pool, 5)
            for k, src in enumerate((stv0, st4, st3, st5, stu3, stu5)):
                for d in range(DT):
                    for o in range(DT):
                        ins = nc.tensor.transpose(ps[:, k, d * D + o * P:d * D + (o + 1) * P],
                                                  src[:, o, d * P:(d + 1) * P], ident[:, :])
                ins.then_inc(q_pe, 1)
            for d in range(DT):
                for e in range(DT):
                    ins = mm(ps[:, 6, d * D:(d + 1) * D], stq0[:, e, d * P:(d + 1) * P], stk0[:, e, :],
                             start=e == 0, stop=e == DT - 1)
            ins.then_inc(q_pe, 1)
            for j in range(PAIRS):
                ins = mm(ps[:, 7, 0:D], bvb[:, j, :], sto[:, j, :], start=j == 0, stop=j == PAIRS - 1)
            ins.then_inc(q_pe, 1)
            pe.wait_ge(q_prep, 33)
            for t in range(NT):
                for s in range(NT):
                    ins = nc.tensor.transpose(ps[:, t, s * P:(s + 1) * P], adj_n[:, s, t * P:(t + 1) * P],
                                              ident[:, :])
                ins.then_inc(q_pe, 1)
            pe.wait_ge(q_prep, Q_PREP_ALL)

            with pe.Fori(0, ITERS) as it:
                v = it + 1
                for l in range(LANES):
                    pe.wait_ge(x_in[l], it * 16 + 16)
                    transpose_nodes(4 * l, xn[:, l]).then_inc(xT_ps[l], 1)
                for l in range(LANES):
                    pe.wait_ge(xT_l[l], v)
                    through(4 * l + 2, W["g0"], HTS[l]).then_inc(y_ps[l], 1)
                for l in range(LANES):
                    pe.wait_ge(y_l[l], v)
                    for t in range(NT):
                        c = slice(t * P, (t + 1) * P)
                        for d in range(DT):
                            ins = mm3(ps[:, 4 * l + t, :], HTS[l][:, H, d, c], HTS[l][:, L, d, c],
                                      AB[l][:, H, d], AB[l][:, L, d], d == 0, d == DT - 1)
                    ins.then_inc(s_ps[l], 1)
                for l in range(LANES):
                    pe.wait_ge(rel_l[l], v)
                    pe.wait_ge(xs_l[l], v)
                    gather(4 * l, XNS[l], RELH[l], RELL[l]).then_inc(u_ps[l], 1)
                for l in range(LANES):
                    pe.wait_ge(u_l[l], v)
                    to_natural(4 * l + 2, AB[l], W["wv0"]).then_inc(o_ps[l], 1)
                    pe.wait_ge(sq_s[l], it * (NT - 1) + (NT - 1))
                    for t in range(NT):
                        ins = mm(ps[:, 4 * l, t:t + 1], REL[l][:, 0, t * P:(t + 1) * P], ones1[:, :],
                                 start=True, stop=True)
                    ins.then_inc(ssq_ps[l], 1)
                for l in range(LANES):
                    pe.wait_ge(x1s_l[l], v)
                    gather(4 * l, XNS[l], adjT[:, H], adjT[:, L]).then_inc(t_ps[l], 1)
                for l in range(LANES):
                    pe.wait_ge(t_l[l], v)
                    to_natural(4 * l + 2, AB[l], W["w1"]).then_inc(o1_ps[l], 1)
                for l in range(LANES):
                    pe.wait_ge(x2_r[l], v)
                    transpose_nodes(4 * l, xn[:, l]).then_inc(hT_ps[l], 1)
                with pe.Fori(0, STEPS) as j:
                    for l in range(LANES):
                        m = it * 6 + j * 2 + (l + 1)
                        o = 1 - l
                        pe.wait_ge(xn_l[l], it * 4 + j + 1)
                        if l == 0:
                            pe.wait_ge(hT_l[0], it * 4 + j + 1)
                        gather(0, XNS[l], adjT[:, H], adjT[:, L]).then_inc(a_ps, 1)
                        pe.wait_ge(hT_l[l], it * 4 + j + 1)
                        pe.wait_ge(z_t, m)
                        through(2, W["u3"], HTS[l], last=False)
                        pe.wait_ge(a_l, m)
                        through(2, W["w4"], AB[0], first=False).then_inc(r_ps, 1)
                        pe.wait_ge(v_t, m)
                        if l == 0:
                            pe.wait_ge(hT_l[1], it * 4 + j + 1)
                        through(4, W["w5"], AB[0], last=False)
                        pe.wait_ge(h_f[o], it * 4 + j + (1 if o == 1 else 2))
                        transpose_features(6, hT[o]).then_inc(tp_ps[o], 1)
                        pe.wait_ge(r_t, m)
                        through(2, W["wd"], AB[0], first=False, again=True).then_inc(z_ps, 1)
                        pe.wait_ge(rh_l, m)
                        through(4, W["u5"], AB[1], first=False).then_inc(v_ps, 1)
                pe.wait_ge(h_f[1], it * 4 + 4)
                transpose_features(6, hT[1]).then_inc(tp_ps[1], 1)
                for l in range(LANES):
                    pe.wait_ge(x3_r[l], v)
                    transpose_nodes(4, xn[:, l]).then_inc(x3_ps[l], 1)
                    pe.wait_ge(x3_l[l], v)
                    if l == 1:
                        pe.wait_ge(q_l[0], v)
                        pe.wait_ge(k_l[0], v)
                    through(0, W["wq"], X3T).then_inc(q_ps[l], 1)
                    through(2, W["wk"], X3T).then_inc(k_ps[l], 1)
                    if l == 0:
                        pe.wait_ge(xn_l[1], it * 4 + 4)
                        to_natural(6, X3T, W["wv"]).then_inc(vv_ps[0], 1)
                pe.wait_ge(q_l[1], v)
                pe.wait_ge(k_l[1], v)
                pe.wait_ge(vv_l[0], v)
                for n in range(-2, HEADJOBS + 1):
                    if 0 <= n < HEADJOBS:
                        pe.wait_ge(nrm, it * QT + (n + 1) * NT)
                        for k in range(NT):
                            if n > 0:
                                pe.wait_ge(pt_l, it * QT + ((n - 1) * NT + k + 1))
                            for q in range(NT):
                                ins = nc.tensor.transpose(ps[:, 4 + k, q * P:(q + 1) * P],
                                                          SC[:, 4 * (n % 2) + q, k * P:(k + 1) * P], ident[:, :])
                            ins.then_inc(pt_ps, 1)
                    if n + 2 < HEADJOBS:
                        s = n + 2
                        pe.wait_ge(stk[s % 4], it * (128 * HEADJOBS // 4) + 128 * (s // 4 + 1))
                        if s == HEADS + 3:
                            pe.wait_ge(vv_l[1], v)
                        for q in range(NT):
                            pe.wait_ge(ttr, it * QT + (s * NT + q + 1))
                            mm(ps[:, (s * NT + q) % 2, :], STK[:, s % 4, 0, q * P:(q + 1) * P], STK[:, s % 4, 1, :],
                               start=True, stop=True).then_inc(sc_ps, 1)
                    if n >= 1:
                        s = n - 1
                        pr = s // 2
                        if s % 2 == 0 and pr % PAIRS >= 2:
                            pe.wait_ge(ot_l, it * (HEADJOBS // 2) + (pr - 1))
                        if s == HEADS:
                            pe.wait_ge(yo_r[0], v)
                            pe.wait_ge(vv_l[1], v)
                        for k in range(NT):
                            pe.wait_ge(pt_l, it * QT + (s * NT + k + 1))
                            mm(ps[:, 2 + pr % 2, :], VP[:, k * PAIRS + pr % PAIRS, s % 2, :], PT[:, k, H],
                               start=s % 2 == 0 and k == 0, stop=False)
                            mm(ps[:, 2 + pr % 2, :], VP[:, k * PAIRS + pr % PAIRS, s % 2, :], PT[:, k, L],
                               start=False, stop=s % 2 == 1 and k == NT - 1).then_inc(pv, 1)
                    if n == HEADS:
                        pe.wait_ge(ttr, it * QT + ((n + 3) * NT + 2))
                        to_natural(0, X3T, W["wv"]).then_inc(vv_ps[1], 1)
                    if n == HEADS or n == HEADJOBS:
                        l = n // HEADS - 1
                        pe.wait_ge(ot_l, it * (HEADJOBS // 2) + n // 2)
                        dst = natural(2)
                        for t in range(NT):
                            c = slice(t * P, (t + 1) * P)
                            for pr in range(PAIRS):
                                k = 2 * (pr % 2)
                                ins = mm3(dst[:, t], SRC[l][:, pr // 2, k + H, c], SRC[l][:, pr // 2, k + L, c],
                                          Wo[:, H, pr], Wo[:, L, pr], pr == 0, pr == PAIRS - 1)
                        ins.then_inc(yo_ps[l], 1)


_INS = ["x", "adj", "L0_gnn_Wq", "L0_gnn_Wk", "L0_gnn_Wv", "L1_gnn_weight", "L1_gnn_bias",
        "L2_gnn_w3_w", "L2_gnn_w3_b", "L2_gnn_u3_w", "L2_gnn_u3_b", "L2_gnn_w4_w", "L2_gnn_w4_b",
        "L2_gnn_w5_w", "L2_gnn_w5_b", "L2_gnn_u5_w", "L2_gnn_u5_b",
        "L3_gnn_Wq", "L3_gnn_bq", "L3_gnn_Wk", "L3_gnn_bk", "L3_gnn_Wv", "L3_gnn_bv", "L3_gnn_Wo", "L3_gnn_bo"]


def kernel(**inputs):
    import concourse.bacc as bacc
    from concourse.bass_utils import run_bass_kernel_spmd

    nc = bacc.Bacc("TRN2", target_bir_lowering=False, num_devices=1)
    arrays, args = {}, []
    for name in _INS:
        a = np.ascontiguousarray(inputs[name])
        arrays[f"in_{name}"] = a
        args.append(nc.dram_tensor(f"in_{name}", a.shape, mybir.dt.from_np(a.dtype), kind="ExternalInput").ap())
    shape = tuple(inputs["x"].shape)
    args.append(nc.dram_tensor("out_0", shape, F32, kind="ExternalOutput").ap())
    gnn_stack(nc, *args)
    r = run_bass_kernel_spmd(nc, [arrays], core_ids=[0])
    return r.results[0]["out_0"]
```

```python
import numpy as np
from contextlib import ExitStack

import concourse.bass as bass
from concourse import mybir

F32 = mybir.dt.float32
F32R = mybir.dt.float32r
ALU = mybir.AluOpType
ACT = mybir.ActivationFunctionType
AX = mybir.AxisListType

P = 128
LANES = 2
STEPS = 3
HEADS = 8
EPS = 1e-5
NEG = 1.0e9


def gnn_stack(nc, x, adj, wq0, wk0, wv0, w1, b1, w3, bw3, u3, bu3, w4, bw4, w5, bw5, u5, bu5,
              wq, bq, wk, bk, wv, bv, wo, bo, out):
    B, N, D = x.shape
    NT = N // P
    DT = D // P
    ITERS = B // LANES
    HD = D // HEADS
    PAIRS = HEADS // 2
    HEADJOBS = LANES * HEADS
    QT = NT * HEADJOBS
    UNIT = 2 * DT * N
    LT = (NT - 1) * HEADJOBS
    RING = 3 * NT
    assert NT * D == DT * N and HD == 32 and N == 512 and D == 256

    xv = x.rearrange("(i l) (t p) d -> l i p t d", l=LANES, p=P)
    ov = out.rearrange("(i l) (t p) d -> l i p t d", l=LANES, p=P)

    with ExitStack() as ctx:
        def sb(name, shape, dt=F32):
            return ctx.enter_context(nc.sbuf_tensor(name, shape, dt))

        def sem(name):
            return ctx.enter_context(nc.semaphore(name))

        def sems(name, n=LANES):
            return [sem(f"{name}{k}") for k in range(n)]

        adj_n = sb("adj_n", [P, NT, N])
        mask = sb("mask", [P, NT, N])
        adjT = sb("adjT", [P, 2, NT, N], F32R)
        wnames = ["g0", "wv0", "w1", "w4", "wd", "w5", "u3", "u5", "wq", "wk", "wv"]
        W = {n: sb(f"W_{n}", [P, 2, DT, D], F32R) for n in wnames}
        Wo = sb("W_o", [P, 2, PAIRS, D], F32R)
        ident = sb("ident", [P, P])
        ones1 = sb("ones1", [P, 1])
        b1row = sb("b1row", [P, D])
        crow = sb("crow", [P, D])
        cols = sb("cols", [P, 10, DT])
        BW3, BU3, BW4, BW5, BU5, BQ, BK, BZ, BR, BH = range(10)
        bv4 = sb("bv4", [P, PAIRS])
        dinv = sb("dinv", [P, NT])
        dtmp = sb("dtmp", [P, 3, NT])
        mhalf = sb("mhalf", [P, 8])
        inexact = sb("inexact", [P, 1])
        any_lo = sb("any_lo", [1, 1], mybir.dt.int32)

        xn = sb("xn", [P, LANES, NT, D])
        stats = sb("stats", [P, LANES, NT, 6])
        mv = sb("mv", [P, LANES, NT, 2])
        veps = sb("veps", [P, LANES, NT])
        rstd = sb("rstd", [P, LANES, NT])
        rsd = sb("rsd", [P, LANES, NT])
        ssq = sb("ssq", [P, LANES, NT])
        rnorm = sb("rnorm", [P, LANES, NT])
        nmax = sb("nmax", [P, RING])
        esum = sb("esum", [P, RING])
        rsum = sb("rsum", [P, RING])
        fa = sb("fa", [P, RING * N])
        ra = sb("ra", [P, 11 * UNIT - N], F32R)
        pt_whole = sb("pt_whole", [P, N])

        def fview(word, a, b):
            return fa[:, word:word + a * b].rearrange("p (a b) -> p a b", a=a)

        def rview(unit, a, b, units=1):
            return ra[:, unit * UNIT:(unit + units) * UNIT].rearrange("p (s a b) -> p s a b", a=a, b=b)

        def f32(v):
            return v.bitcast(F32)

        H, L = 0, 1
        XNS = [rview(0, NT, D), rview(1, NT, D)]
        HTS = [rview(2, DT, N), rview(3, DT, N)]
        AB = [rview(4, DT, N), rview(5, DT, N)]
        RELH = [ra[:, (2 + l) * UNIT:(3 + l) * UNIT].rearrange("p (a b) -> p a b", a=NT) for l in range(2)]
        RELL = [ra[:, (4 + l) * UNIT:(5 + l) * UNIT].rearrange("p (a b) -> p a b", a=NT) for l in range(2)]
        STK = rview(0, 2, N, units=2)
        SRC = [rview(2, 4, N, units=2), rview(4, 4, N, units=2)]
        VP = ra[:, 6 * UNIT:8 * UNIT].rearrange("p (a e c) -> p a e c", e=2, c=P)
        X3T = rview(8, DT, N)
        PT = ra[:, 9 * UNIT:].rearrange("p (s b) -> p s b", b=N)
        REL = [fview(0, NT, N), fview(NT * N, NT, N)]
        XS = [fview(0, NT, D), fview(NT * N, NT, D)]
        hT = [fview(0, DT, N), fview(DT * N, DT, N)]
        tr, tz, thv = [fview((2 + k) * DT * N, DT, N) for k in range(3)]
        SC = fview(0, RING, N)
        XIN = [fview(2 * NT * N + l * NT * D, NT, D) for l in range(LANES)]
        assert (HEADJOBS - 2) % 3 == 2

        ps = ctx.enter_context(nc.psum_tensor("ps", [P, 8, N], F32))

        def pair(b):
            return ps[:, b:b + 2, :]

        Y = (6, 4)

        def natural(b):
            return ps[:, b:b + 2, :].rearrange("p b (t d) -> p (b t) d", d=D)

        q_w = sem("setup_loads"); q_adj = sem("setup_adj_load"); q_prep = sem("setup_dve")
        q_act = sem("setup_act"); q_pe = sem("setup_pe"); q_pool = sem("setup_pool")
        c_dve = sem("dve_chain")
        x_in = sems("x_loaded"); out_done = sems("out_stored")
        xT_ps = sems("xT_ps"); xT_h = sems("xT_h"); xT_l = sems("xT_l")
        xs_h = sems("x_split_h"); xs_l = sems("x_split")
        y_ps = sems("y_ps"); y_h = sems("y_h"); y_l = sems("y_l")
        s_ps = sems("gram_ps"); rel_f = sems("rel_masked"); rel_h = sems("rel_h"); rel_l = sems("rel_l")
        sq_f = sems("rel_squared"); sq_s = sems("squares_summed"); ssq_ps = sems("ssq_ps")
        ssq_c = sems("ssq_copied"); rn_r = sems("rnorm_ready")
        u_ps = sems("u_ps"); u_h = sems("u_h"); u_l = sems("u_l"); o_ps = sems("o_ps")
        ln_v = sems("ln_var"); ln_r = sems("ln_rstd")
        x1s_f = sems("x1_scaled"); x1s_h = sems("x1s_h"); x1s_l = sems("x1s_l"); xb_r = sems("x1_plus_bias")
        t_ps = sems("t_ps"); t_h = sems("t_h"); t_l = sems("t_l"); o1_ps = sems("o1_ps")
        x2_r = sems("x2_ready")
        hT_ps = sems("hT_ps"); hT_h = sems("hT_h")
        h_f = sems("h_ready"); hT_l = sems("hT_l")
        xn_h = sems("hn_h"); xn_l = sems("hn_l")
        tp_ps = sems("hn_ps")
        a_ps = sem("a_ps"); a_h = sem("a_h"); a_l = sem("a_l")
        r_ps = sem("r_ps"); r_t = sem("r_tanh"); z_ps = sem("z_ps"); z_t = sem("z_tanh")
        v_ps = sem("hv_ps"); v_t = sem("hv_tanh"); rh_l = sem("rh_l")
        x3_r = sems("x3_ready"); x3_ps = sems("x3T_ps"); x3_h = sems("x3T_h"); x3_l = sems("x3T_l")
        q_ps = sems("q_ps"); k_ps = sems("k_ps"); vv_ps = sems("v_ps")
        q_h = sems("q_h"); k_h = sems("k_h"); vv_h = sems("v_h")
        q_l = sems("q_l"); k_l = sems("k_l"); vv_l = sems("v_l")
        stk = sems("stacked", 4)
        sc_ps = sem("score_ps"); ttr = sem("score_masked"); ex = sem("score_exp"); nrm = sem("prob_ready")
        rs_r = sem("row_sum_inverted")
        pt_ps = sem("probT_ps"); pt_h = sem("probT_h"); pt_l = sem("probT_l"); pv = sem("pv_done")
        ot_h = sem("ot_h"); ot_l = sem("ot_l")
        yo_ps = sems("attn_out_ps"); yo_r = sems("attn_out_read"); xc_r = sems("x3_plus_const")
        x4_r = sems("x4_ready")

        CHAIN = 50
        Q_PREP_ALL, Q_PE_ALL = 43, 13

        gates = {"dve": sem("dve_gate"), "pool": sem("pool_gate"), "sp": sem("sp_gate")}

        def settle(eng, who):
            eng.sem_inc(gates[who], 1)

        block = ctx.enter_context(nc.Block())

        st3, st4, st5 = [fview(k * DT * 2 * D, DT, 2 * D) for k in range(3)]
        stu3, stu5, stv0, stk0 = [fview(3 * DT * 2 * D + k * DT * D, DT, D) for k in range(4)]
        stq0, st1 = [xn[:, 0, 2 * k:2 * k + 2, :] for k in range(2)]
        sto = xn[:, 1, :, :]
        stq, stkk, stvv = [mask[:, k, :].rearrange("p (a b) -> p a b", a=DT) for k in range(3)]
        bvb = mask[:, 3, :].rearrange("p (a b) -> p a b", a=PAIRS)

        @block.sync
        def _(sp):
            def rows(ap):
                return ap.rearrange("(t p) d -> p t d", p=P)

            sp.dma_start(adj_n[:, :, :], rows(adj)).then_inc(q_adj, 16)
            for dst, src in ((st3, w3), (st4, w4), (st5, w5), (stu3, u3), (stu5, u5), (stv0, wv0),
                             (stk0, wk0), (stq0, wq0), (st1, w1), (stq, wq), (stkk, wk), (stvv, wv)):
                sp.dma_start(dst, rows(src)).then_inc(q_w, 16)
            wo_rows = wo.rearrange("(j e p) d -> e p j d", e=2, p=HD)
            bv_rows = bv.rearrange("(j e p) -> e p j", e=2, p=HD)
            for e in range(2):
                for c in range(2):
                    part = (2 * e + c) * HD
                    sp.dma_start(sto[part:part + HD, :, :], wo_rows[e]).then_inc(q_w, 16)
                    with nc.allow_non_contiguous_dma("a few words of bias"):
                        sp.dma_start(bv4[part:part + HD, :], bv_rows[e]).then_inc(q_w, 16)
            with nc.allow_non_contiguous_dma("a few words of bias"):
                for k, src in ((BW3, bw3), (BU3, bu3), (BW4, bw4), (BW5, bw5), (BU5, bu5), (BQ, bq), (BK, bk)):
                    sp.dma_start(cols[:, k, :], src.rearrange("(t p) -> p t", p=P)).then_inc(q_w, 16)
            sp.dma_start(b1row[:, :], b1.rearrange("(a d) -> a d", a=1).broadcast_to((P, D))).then_inc(q_w, 16)
            sp.dma_start(crow[:, :], bo.rearrange("(a d) -> a d", a=1).broadcast_to((P, D))).then_inc(q_w, 16)
            for l in range(LANES):
                sp.sem_inc(out_done[l], 16)

            with sp.Fori(0, ITERS) as it:
                for n in range(HEADJOBS):
                    l, h, slot = n // HEADS, n % HEADS, n % 4
                    if h == 0:
                        sp.wait_ge(q_l[l], it + 1)
                        sp.wait_ge(k_l[l], it + 1)
                        settle(sp, "sp")
                    if n >= 4:
                        sp.wait_ge(sc_ps, it * QT + (n - 3) * NT)
                    g, r = h // 4, (h % 4) * HD
                    for c, parts in enumerate((slice(0, 3, 2), slice(1, 4, 2), slice(0, 4, 3), slice(1, 3, 1))):
                        sp.dma_start(f32(STK[c * HD:(c + 1) * HD, slot, :, :]),
                                     f32(SRC[l][r:r + HD, g, parts, :])).then_inc(stk[slot], 16)
                    if n == HEADS + 5:
                        sp.wait_ge(x4_r[0], it + 1)
                        settle(sp, "sp")
                        sp.dma_start(ov[0][it], xn[:, 0, :, :]).then_inc(out_done[0], 16)
                sp.wait_ge(x4_r[1], it + 1)
                settle(sp, "sp")
                sp.dma_start(ov[1][it], xn[:, 1, :, :]).then_inc(out_done[1], 16)
            for l in range(LANES):
                sp.wait_ge(out_done[l], 16 * (ITERS + 1))

        @block.gpsimd
        def _(gp):
            nc.gpsimd.memset(ident[:, :], 0.0).then_inc(q_pool, 1)
            nc.gpsimd.memset(mhalf[:, 0:4], -0.5).then_inc(q_pool, 1)
            nc.gpsimd.memset(mhalf[:, 4:8], -1.0).then_inc(q_pool, 1)
            nc.gpsimd.memset(ones1[:, :], 1.0).then_inc(q_pool, 1)
            gp.wait_ge(q_pool, 4)
            nc.gpsimd.affine_select(out=ident[:, :], in_=ident[:, :], compare_op=ALU.not_equal, fill=1.0,
                                    base=0, pattern=[[-1, P]], channel_multiplier=1).then_inc(q_pool, 1)
            gp.wait_ge(q_prep, 2)
            nc.gpsimd.tensor_tensor(dtmp[:, 2, :], dtmp[:, 1, :], mhalf[:, 0:NT], ALU.pow).then_inc(q_pool, 1)

            def load_x(l, i, k):
                settle(gp, "pool")
                gp.dma_start(XIN[l], xv[l][i]).then_inc(x_in[l], 16)

            def split_x(l, k):
                gp.wait_ge(x_in[l], 16 * k + 16)
                settle(gp, "pool")
                nc.gpsimd.tensor_scalar(XNS[l][:, H], XIN[l], 1.0, 1.0, ALU.mult, ALU.mult).then_inc(xs_h[l], 1)
                gp.wait_ge(xs_h[l], k + 1)
                nc.gpsimd.tensor_tensor(XNS[l][:, L], XIN[l], f32(XNS[l][:, H]), ALU.subtract).then_inc(xs_l[l], 1)

            gp.wait_ge(q_pe, 7)
            for l in range(LANES):
                load_x(l, 0, 0)
            for l in range(LANES):
                split_x(l, 0)

            with gp.Fori(0, ITERS) as it:
                def rstd_of(l, k):
                    gp.wait_ge(ln_v[l], it * 4 + (k + 1))
                    nc.gpsimd.tensor_tensor(rstd[:, l, :], veps[:, l, :], mhalf[:, 0:NT],
                                            ALU.pow).then_inc(ln_r[l], 1)

                def squares(l):
                    gp.wait_ge(sq_f[l], it + 1)
                    for t in range(1, NT):
                        nc.gpsimd.tensor_tensor(REL[l][:, 0], REL[l][:, 0], REL[l][:, t],
                                                ALU.add).then_inc(sq_s[l], 1)
                        if t < NT - 1:
                            gp.wait_ge(sq_s[l], it * (NT - 1) + t)

                def rnorm_of(l):
                    gp.wait_ge(ssq_c[l], it + 1)
                    nc.gpsimd.tensor_tensor(rnorm[:, l, :], ssq[:, l, :], mhalf[:, 0:NT],
                                            ALU.pow).then_inc(rn_r[l], 1)

                def add_row(l, row, signal):
                    for t in range(NT):
                        ins = nc.gpsimd.tensor_tensor(xn[:, l, t], xn[:, l, t], row[:, :], ALU.add)
                    ins.then_inc(signal[l], 1)

                squares(0)
                rnorm_of(0)
                rstd_of(0, 0)
                squares(1)
                rnorm_of(1)
                gp.wait_ge(x1s_f[0], it + 1)
                add_row(0, b1row, xb_r)
                rstd_of(1, 0)
                gp.wait_ge(x1s_f[1], it + 1)
                add_row(1, b1row, xb_r)
                rstd_of(0, 1)
                rstd_of(1, 1)
                rstd_of(0, 2)
                rstd_of(1, 2)
                for l in range(LANES):
                    gp.wait_ge(x3_ps[l], it + 1)
                    add_row(l, crow, xc_r)
                for n in range(HEADJOBS):
                    gp.wait_ge(ex, it * QT + (n + 1) * NT)
                    s0 = (n % 3) * NT
                    nc.gpsimd.tensor_tensor(rsum[:, s0:s0 + NT], esum[:, s0:s0 + NT], mhalf[:, 4:4 + NT],
                                            ALU.pow).then_inc(rs_r, 1)
                    gp.wait_ge(rs_r, it * HEADJOBS + (n + 1))
                    settle(gp, "pool")
                    for t in range(NT):
                        nc.gpsimd.tensor_scalar(SC[:, s0 + t], SC[:, s0 + t], rsum[:, s0 + t:s0 + t + 1], 1.0,
                                                ALU.mult, ALU.mult).then_inc(nrm, 1)
                    if n == HEADS + 3:
                        rstd_of(0, 3)
                gp.wait_ge(pt_ps, it * QT + (QT - NT))
                for l in range(LANES):
                    load_x(l, (it + 1) % ITERS, it + 1)
                gp.wait_ge(sc_ps, it * QT + QT)
                for l in range(LANES):
                    split_x(l, it + 1)
                rstd_of(1, 3)

        @block.scalar
        def _(act):
            def copy(dst, src):
                return nc.scalar.copy(dst, src)

            def xT_hi(l, k):
                act.wait_ge(xT_ps[l], k + 1)
                copy(HTS[l][:, H], pair(4 * l)).then_inc(xT_h[l], 1)

            def y_hi(l, k):
                act.wait_ge(y_ps[l], k + 1)
                copy(AB[l][:, H], pair(Y[l])).then_inc(y_h[l], 1)

            act.wait_ge(q_prep, 12)
            copy(W["w1"][:, H], st1).then_inc(q_act, 1)
            copy(W["wq"][:, H], stq).then_inc(q_act, 1)
            copy(W["wk"][:, H], stkk).then_inc(q_act, 1)
            copy(W["wv"][:, H], stvv).then_inc(q_act, 1)
            copy(Wo[:, H], sto).then_inc(q_act, 1)
            for k, name in enumerate(["wv0", "w4", "wd", "w5", "u3", "u5", "g0"]):
                act.wait_ge(q_pe, k + 1)
                copy(W[name][:, H], ps[:, k, :].rearrange("p (a b) -> p a b", a=DT)).then_inc(q_act, 1)
            for t in range(NT):
                act.wait_ge(q_pe, 9 + t)
                copy(adjT[:, H, t], ps[:, t, :]).then_inc(q_act, 1)

            act.sem_inc(z_t, 1)
            act.sem_inc(v_t, 1)
            for l in range(LANES):
                xT_hi(l, 0)
            for l in range(LANES):
                y_hi(l, 0)

            with act.Fori(0, ITERS) as it:
                v = it + 1

                def hi(dst, src, ready, signal, value=None):
                    act.wait_ge(ready, v if value is None else value)
                    copy(dst, src).then_inc(signal, 1)

                def rel_hi(l):
                    for c in range(2):
                        t = slice(2 * c, 2 * c + 2)
                        hi(RELH[l][:, t], REL[l][:, t], rel_f[l], rel_h[l], it * 2 + (c + 1))

                def square(l):
                    act.wait_ge(rel_l[l], v)
                    nc.scalar.activation(REL[l][:, :, :], REL[l][:, :, :], ACT.Square).then_inc(sq_f[l], 1)

                rel_hi(0)
                square(0)
                rel_hi(1)
                hi(AB[0][:, H], pair(0), u_ps[0], u_h[0], it * 2 + 2)
                square(1)
                hi(AB[1][:, H], pair(4), u_ps[1], u_h[1], it * 2 + 2)
                hi(XNS[0][:, H], XS[0], x1s_f[0], x1s_h[0])
                hi(AB[0][:, H], pair(0), t_ps[0], t_h[0])
                hi(XNS[1][:, H], XS[1], x1s_f[1], x1s_h[1])
                hi(AB[1][:, H], pair(4), t_ps[1], t_h[1])
                hi(XNS[0][:, H], xn[:, 0], x2_r[0], xn_h[0])
                hi(HTS[0][:, H], pair(0), hT_ps[0], hT_h[0])
                for j in range(STEPS):
                    for l in range(LANES):
                        m = it * 6 + (j * 2 + l + 1)
                        o = 1 - l
                        hi(AB[0][:, H], pair(0), a_ps, a_h, m)
                        if j + l > 0 and not (l == 1 and j == STEPS - 1):
                            hi(HTS[o][:, H], hT[o], h_f[o], hT_h[o], it * 4 + (j + 1 + l))
                        if j + l > 0 and not (l == 1 and j == STEPS - 1):
                            hi(XNS[o][:, H], natural(6), tp_ps[o], xn_h[o], it * 3 + (j + l))
                        act.wait_ge(r_ps, m)
                        for d in range(DT):
                            ins = nc.scalar.activation(tr[:, d], ps[:, 2 + d], ACT.Tanh,
                                                       bias=cols[:, BR, d:d + 1], scale=0.5)
                        ins.then_inc(r_t, 1)
                        if l == 0 and j == 0:
                            hi(XNS[1][:, H], xn[:, 1], x2_r[1], xn_h[1])
                            hi(HTS[1][:, H], pair(6), hT_ps[1], hT_h[1])
                        act.wait_ge(z_ps, m)
                        for d in range(DT):
                            ins = nc.scalar.activation(tz[:, d], ps[:, 2 + d], ACT.Tanh,
                                                       bias=cols[:, BZ, d:d + 1], scale=0.5)
                        ins.then_inc(z_t, 1)
                        if l == 1 and j == STEPS - 1:
                            hi(X3T[:, H], pair(0), x3_ps[0], x3_h[0])
                        act.wait_ge(v_ps, m)
                        for d in range(DT):
                            ins = nc.scalar.activation(thv[:, d], ps[:, 4 + d], ACT.Tanh,
                                                       bias=cols[:, BH, d:d + 1])
                        ins.then_inc(v_t, 1)

                def proj_hi(sem_ps, sem_h, l, b, k, bias):
                    act.wait_ge(sem_ps[l], v)
                    for d in range(DT):
                        ins = nc.scalar.activation(SRC[l][:, d, 2 * k], ps[:, b + d], ACT.Identity,
                                                   bias=cols[:, bias, d:d + 1])
                    ins.then_inc(sem_h[l], 1)

                def v_hi(l, b):
                    act.wait_ge(vv_ps[l], v)
                    src = natural(b).rearrange("p t (j e c) -> p (t j) e c", e=2, c=HD)
                    copy(VP[:, :, 0, 0:HD], src[:, :, 0])
                    copy(VP[:, :, 1, 2 * HD:3 * HD], src[:, :, 1]).then_inc(vv_h[l], 1)

                proj_hi(q_ps, q_h, 0, 2, 0, BQ)
                proj_hi(k_ps, k_h, 0, 4, 1, BK)
                v_hi(0, 0)
                for n in range(-2, HEADJOBS + 1):
                    if n == -1:
                        proj_hi(q_ps, q_h, 1, 4, 0, BQ)
                        proj_hi(k_ps, k_h, 1, 6, 1, BK)

                    def prob_hi(q):
                        if 0 <= n < HEADJOBS:
                            if n > 0:
                                act.wait_ge(pv, it * QT + ((n - 1) * NT + q + 1))
                            hi(PT[:, 2 * q + H] if q < NT - 1 else pt_whole[:, :], ps[:, 4 + q], pt_ps, pt_h, it * QT + (n * NT + q + 1))

                    def exponentials(q):
                        if n + 2 < HEADJOBS:
                            g = ((n + 2) * NT + q) % RING
                            act.wait_ge(ttr, it * QT + ((n + 2) * NT + q + 1 + 2))
                            nc.scalar.activation(SC[:, g], SC[:, g], ACT.Exp, bias=nmax[:, g:g + 1], scale=-1.0,
                                                 accum_out=esum[:, g:g + 1]).then_inc(ex, 1)

                    prob_hi(0)
                    prob_hi(1)
                    exponentials(0)
                    if n == -2:
                        hi(X3T[:, H], pair(6), x3_ps[1], x3_h[1])
                    prob_hi(2)
                    exponentials(1)
                    prob_hi(3)
                    exponentials(2)
                    exponentials(3)
                    if n >= 2 and n % 2 == 0:
                        pr = n // 2 - 1
                        hi(SRC[pr // PAIRS][:, (pr % PAIRS) // 2, 2 * (pr % 2) + H], ps[:, 2 + pr % 2],
                           pv, ot_h, it * QT + n * NT)
                    if n == HEADS:
                        v_hi(1, 0)
                for l in range(LANES):
                    xT_hi(l, it + 1)
                for l in range(LANES):
                    y_hi(l, it + 1)

        @block.vector
        def _(dve):
            TT, STT, TS = nc.vector.tensor_tensor, nc.vector.scalar_tensor_tensor, nc.vector.tensor_scalar
            steps = [0]

            def prep(ins):
                steps[0] += 1
                ins.then_inc(q_prep, 1)
                dve.wait_ge(q_prep, steps[0])

            dve.wait_ge(q_adj, 16)
            prep(nc.vector.reduce_sum(dtmp[:, 0, :], adj_n[:, :, :], AX.X))
            prep(TS(dtmp[:, 1, :], dtmp[:, 0, :], 1.2e-38, None, ALU.max))
            dve.wait_ge(q_w, 16 * (12 + 8 + 7 + 2))
            prep(TT(st3[:, :, 0:D], st3[:, :, 0:D], st3[:, :, D:2 * D], ALU.add))
            prep(TT(st4[:, :, 0:D], st4[:, :, 0:D], st4[:, :, D:2 * D], ALU.add))
            prep(TT(st5[:, :, 0:D], st5[:, :, 0:D], st5[:, :, D:2 * D], ALU.add))
            prep(TT(st3[:, :, 0:D], st3[:, :, 0:D], st4[:, :, 0:D], ALU.subtract))
            prep(TS(stu5, stu5, 0.5, None, ALU.mult))
            prep(TS(stq, stq, float(HD) ** -0.5, None, ALU.mult))
            prep(TS(cols[:, BQ, :], cols[:, BQ, :], float(HD) ** -0.5, None, ALU.mult))
            prep(TT(cols[:, BZ, :], cols[:, BW3, :], cols[:, BU3, :], ALU.add))
            prep(TT(cols[:, BR, :], cols[:, BW4, :], cols[:, BU3, :], ALU.add))
            prep(TT(cols[:, BH, :], cols[:, BW5, :], cols[:, BU5, :], ALU.add))
            prep(TS(cols[:, BZ, :], cols[:, BZ, :], 0.5, None, ALU.mult))
            prep(TS(cols[:, BR, :], cols[:, BR, :], 0.5, None, ALU.mult))
            dve.wait_ge(q_pool, 5)
            for j in range(PAIRS):
                prep(TS(bvb[:, j, :], ident[:, :], 0.0, bv4[:, j:j + 1], ALU.mult, ALU.add))
            prep(TS(bvb[:, :, :], bvb[:, :, :], 0.5, None, ALU.mult))
            dve.wait_ge(q_pool, 6)
            prep(TS(dtmp[:, 0, :], dtmp[:, 0, :], 0.0, None, ALU.is_gt))
            prep(TT(dinv[:, :], dtmp[:, 0, :], dtmp[:, 2, :], ALU.mult))
            n_act = 0
            for dst, src in (("w1", st1), ("wq", stq), ("wk", stkk), ("wv", stvv)):
                n_act += 1
                dve.wait_ge(q_act, n_act)
                prep(TT(W[dst][:, L], src, f32(W[dst][:, H]), ALU.subtract))
            n_act += 1
            dve.wait_ge(q_act, n_act)
            prep(TT(Wo[:, L], sto, f32(Wo[:, H]), ALU.subtract))
            for k, name in enumerate(["wv0", "w4", "wd", "w5", "u3", "u5", "g0"]):
                n_act += 1
                dve.wait_ge(q_act, n_act)
                prep(TT(W[name][:, L], ps[:, k, :].rearrange("p (a b) -> p a b", a=DT), f32(W[name][:, H]),
                        ALU.subtract))
            dve.wait_ge(q_pe, 8)
            prep(TT(crow[:, :], crow[:, :], ps[:, 7, 0:D], ALU.add))
            for t in range(NT):
                n_act += 1
                dve.wait_ge(q_act, n_act)
                prep(TT(adjT[:, L, t], ps[:, t, :], f32(adjT[:, H, t]), ALU.subtract))
            prep(TS(REL[0], f32(adjT[:, L]), 0.0, None, ALU.not_equal))
            prep(nc.vector.reduce_sum(inexact[:, :], fa[:, 0:NT * N], AX.X))
            prep(TS(mask[:, :, :], adj_n[:, :, :], 1.0, NEG, ALU.subtract, ALU.mult))
            prep(nc.vector.memset(f32(ra[:, 6 * UNIT:8 * UNIT]), 0.0))
            dve.wait_ge(q_pe, 8 + NT + 1)
            prep(nc.vector.tensor_copy(any_lo[:, :], ps[0:1, 7, 0:1]))
            assert steps[0] == Q_PREP_ALL

            for _ in range(2):
                dve.sem_inc(ttr, 1)

            def xT_lo(l, k):
                dve.wait_ge(xT_h[l], k + 1)
                TT(HTS[l][:, L], pair(4 * l), f32(HTS[l][:, H]), ALU.subtract).then_inc(xT_l[l], 1)

            def y_lo(l, k):
                dve.wait_ge(y_h[l], k + 1)
                TT(AB[l][:, L], pair(Y[l]), f32(AB[l][:, H]), ALU.subtract).then_inc(y_l[l], 1)

            for l in range(LANES):
                xT_lo(l, 0)
            for l in range(LANES):
                y_lo(l, 0)

            with dve.Fori(0, ITERS) as it:
                v = it + 1
                done = [0]

                def link(ins):
                    done[0] += 1
                    ins.then_inc(c_dve, 1)
                    dve.wait_ge(c_dve, it * CHAIN + done[0])

                def lo(dst, src, hi, wait_sem, value, signal):
                    dve.wait_ge(wait_sem, value)
                    TT(dst, src, f32(hi), ALU.subtract).then_inc(signal, 1)

                def statistics(l):
                    for t in range(NT):
                        ins = nc.vector.bn_stats(stats[:, l, t, :], xn[:, l, t, :])
                    link(ins)
                    settle(dve, "dve")
                    for t in range(NT):
                        ins = nc.vector.bn_aggr(mv[:, l, t, :], stats[:, l, t, :])
                    link(ins)
                    TS(veps[:, l, :], mv[:, l, :, 1], EPS, None, ALU.add).then_inc(ln_v[l], 1)

                def normalize(l, k, signal):
                    dve.wait_ge(ln_r[l], it * 4 + (k + 1))
                    if k == 0:
                        link(TT(rsd[:, l, :], rstd[:, l, :], dinv[:, :], ALU.mult))
                        for t in range(NT):
                            ins = TS(XS[l][:, t], xn[:, l, t], mv[:, l, t, 0:1], rsd[:, l, t:t + 1],
                                     ALU.subtract, ALU.mult)
                        link(ins)
                    for t in range(NT):
                        ins = TS(xn[:, l, t], xn[:, l, t], mv[:, l, t, 0:1], rstd[:, l, t:t + 1],
                                 ALU.subtract, ALU.mult)
                    ins.then_inc(signal[l], 1)

                def residual(l, b, scale, x):
                    for t in range(NT):
                        ins = STT(xn[:, l, t], natural(b)[:, t], scale[:, t:t + 1], x[:, t],
                                  ALU.mult, ALU.add)
                    link(ins)

                def rel_of(l):
                    dve.wait_ge(s_ps[l], v)
                    for c in range(2):
                        t = slice(2 * c, 2 * c + 2)
                        TT(REL[l][:, t], pair(4 * l + 2 * c), adj_n[:, t], ALU.mult).then_inc(rel_f[l], 1)
                    for c in range(2):
                        t = slice(2 * c, 2 * c + 2)
                        dve.wait_ge(rel_h[l], it * 2 + (c + 1))
                        ins = TT(RELL[l][:, t], REL[l][:, t], f32(RELH[l][:, t]), ALU.subtract)
                    ins.then_inc(rel_l[l], 1)

                def after_layer_0(l):
                    dve.wait_ge(ssq_ps[l], v)
                    nc.vector.tensor_copy(ssq[:, l, :], ps[:, 4 * l, 0:NT]).then_inc(ssq_c[l], 1)
                    dve.wait_ge(rn_r[l], v)
                    dve.wait_ge(o_ps[l], v)
                    dve.wait_ge(out_done[l], it * 16 + 16)
                    residual(l, 4 * l + 2, rnorm[:, l], XIN[l])
                    statistics(l)

                def after_layer_1(l):
                    dve.wait_ge(o1_ps[l], v)
                    dve.wait_ge(xb_r[l], v)
                    residual(l, 4 * l + 2, dinv, xn[:, l])
                    statistics(l)
                    normalize(l, 1, x2_r)

                def enter_layer_2(l, b):
                    dve.wait_ge(hT_h[l], it * 3 + 1)
                    nc.vector.tensor_copy(hT[l], pair(b)).then_inc(h_f[l], 1)
                    TT(HTS[l][:, L], pair(b), f32(HTS[l][:, H]), ALU.subtract).then_inc(hT_l[l], 1)

                rel_of(0)
                rel_of(1)
                lo(AB[0][:, L], pair(0), AB[0][:, H], u_h[0], v, u_l[0])
                after_layer_0(0)
                lo(AB[1][:, L], pair(4), AB[1][:, H], u_h[1], v, u_l[1])
                normalize(0, 0, x1s_f)
                lo(XNS[0][:, L], XS[0], XNS[0][:, H], x1s_h[0], v, x1s_l[0])
                after_layer_0(1)
                lo(AB[0][:, L], pair(0), AB[0][:, H], t_h[0], v, t_l[0])
                normalize(1, 0, x1s_f)
                lo(XNS[1][:, L], XS[1], XNS[1][:, H], x1s_h[1], v, x1s_l[1])
                after_layer_1(0)
                lo(AB[1][:, L], pair(4), AB[1][:, H], t_h[1], v, t_l[1])
                lo(XNS[0][:, L], xn[:, 0], XNS[0][:, H], xn_h[0], it * 3 + 1, xn_l[0])
                enter_layer_2(0, 0)
                after_layer_1(1)
                def after_layer_2(l, count):
                    dve.wait_ge(tp_ps[l], count)
                    link(TT(xn[:, l], natural(6), xn[:, l], ALU.add))
                    statistics(l)

                for j in range(STEPS):
                    for l in range(LANES):
                        m = it * 6 + (j * 2 + l + 1)
                        o = 1 - l
                        last = l == 1 and j == STEPS - 1
                        lo(AB[0][:, L], pair(0), AB[0][:, H], a_h, m, a_l)
                        if j + l > 0 and not last:
                            lo(HTS[o][:, L], hT[o], HTS[o][:, H], hT_h[o], it * 3 + (j + 1 + l), hT_l[o])
                            lo(XNS[o][:, L], natural(6), XNS[o][:, H], xn_h[o], it * 3 + (j + 1 + l), xn_l[o])
                        if last:
                            after_layer_2(0, it * 3 + 3)
                        dve.wait_ge(r_t, m)
                        link(STT(tr, tr, 1.0, hT[l], ALU.add, ALU.mult))
                        link(nc.vector.tensor_copy(AB[1][:, H], tr))
                        TT(AB[1][:, L], tr, f32(AB[1][:, H]), ALU.subtract).then_inc(rh_l, 1)
                        if l == 0 and j == 0:
                            lo(XNS[1][:, L], xn[:, 1], XNS[1][:, H], xn_h[1], it * 3 + 1, xn_l[1])
                            enter_layer_2(1, 6)
                        if last:
                            normalize(0, 2, x3_r)
                            lo(X3T[:, L], pair(0), X3T[:, H], x3_h[0], v, x3_l[0])
                        dve.wait_ge(v_t, m + 1)
                        link(TT(thv, thv, hT[l], ALU.subtract))
                        dve.wait_ge(z_t, m + 1)
                        link(STT(tz, tz, 1.0, thv, ALU.add, ALU.mult))
                        STT(hT[l], tz, 0.5, hT[l], ALU.mult, ALU.add).then_inc(h_f[l], 1)

                def proj_lo(sem_h, sem_l, l, b, k, bias):
                    dve.wait_ge(sem_h[l], v)
                    for d in range(DT):
                        ins = STT(SRC[l][:, d, 2 * k + L], ps[:, b + d], cols[:, bias, d:d + 1],
                                  f32(SRC[l][:, d, 2 * k]), ALU.add, ALU.subtract)
                    ins.then_inc(sem_l[l], 1)

                def v_lo(l, b):
                    dve.wait_ge(vv_h[l], v)
                    src = natural(b).rearrange("p t (j e c) -> p (t j) e c", e=2, c=HD)
                    TT(VP[:, :, 0, HD:2 * HD], src[:, :, 0], f32(VP[:, :, 0, 0:HD]), ALU.subtract)
                    TT(VP[:, :, 1, 3 * HD:4 * HD], src[:, :, 1], f32(VP[:, :, 1, 2 * HD:3 * HD]),
                       ALU.subtract).then_inc(vv_l[l], 1)

                def after_layer_3(l):
                    dve.wait_ge(yo_ps[l], v)
                    dve.wait_ge(xc_r[l], v)
                    TT(xn[:, l], natural(2), xn[:, l], ALU.add).then_inc(yo_r[l], 1)

                proj_lo(q_h, q_l, 0, 2, 0, BQ)
                proj_lo(k_h, k_l, 0, 4, 1, BK)
                after_layer_2(1, it * 3 + 3)
                v_lo(0, 0)
                normalize(1, 2, x3_r)
                for n in range(-2, HEADJOBS + 1):
                    if n == -1:
                        proj_lo(q_h, q_l, 1, 4, 0, BQ)
                        proj_lo(k_h, k_l, 1, 6, 1, BK)

                    def masked(q):
                        if n + 2 < HEADJOBS:
                            g = ((n + 2) * NT + q) % RING
                            dve.wait_ge(sc_ps, it * QT + ((n + 2) * NT + q + 1))
                            if n >= 1 and q == 0:
                                dve.wait_ge(pt_ps, it * QT + n * NT)
                            settle(dve, "dve")
                            nc.vector.tensor_tensor_reduce(
                                out=SC[:, g], in0=ps[:, ((n + 2) * NT + q) % 2], in1=mask[:, q], scale=-1.0,
                                scalar=3.0e38, op0=ALU.add, op1=ALU.min, accum_out=nmax[:, g:g + 1]
                            ).then_inc(ttr, 1)

                    def prob_lo(q):
                        if 0 <= n < HEADJOBS:
                            lo(PT[:, 2 * q + L], ps[:, 4 + q], PT[:, 2 * q + H], pt_h, it * QT + (n * NT + q + 1), pt_l)

                    masked(0)
                    masked(1)
                    if n == -2:
                        lo(X3T[:, L], pair(6), X3T[:, H], x3_h[1], v, x3_l[1])
                    prob_lo(0)
                    masked(2)
                    prob_lo(1)
                    masked(3)
                    prob_lo(2)
                    if n >= 2 and n % 2 == 0:
                        pr = n // 2 - 1
                        tile, k = (pr % PAIRS) // 2, 2 * (pr % 2)
                        lo(SRC[pr // PAIRS][:, tile, k + L], ps[:, 2 + pr % 2], SRC[pr // PAIRS][:, tile, k + H],
                           ot_h, it * (HEADJOBS // 2) + (pr + 1), ot_l)
                    if n == HEADS:
                        v_lo(1, 0)
                        after_layer_3(0)
                    if n == HEADS + 1:
                        dve.wait_ge(yo_r[0], v)
                        statistics(0)
                    if n == HEADS + 2:
                        normalize(0, 3, x4_r)
                for l in range(LANES):
                    xT_lo(l, it + 1)
                after_layer_3(1)
                dve.wait_ge(yo_r[1], v)
                statistics(1)
                y_lo(0, it + 1)
                normalize(1, 3, x4_r)
                y_lo(1, it + 1)
                assert done[0] == CHAIN, done

        @block.tensor
        def _(pe):
            mm = nc.tensor.matmul

            def mm3(dst, w_h, w_l, m_h, m_l, first, last, again=False):
                mm(dst, w_h, m_h, start=first, stop=False, skip_group_check=again)
                mm(dst, w_l, m_h, start=False, stop=False, skip_group_check=again)
                return mm(dst, w_h, m_l, start=False, stop=last, skip_group_check=again)

            def through(b, w, src, first=True, last=True, again=False):
                for o in range(DT):
                    c = slice(o * P, (o + 1) * P)
                    for d in range(DT):
                        ins = mm3(ps[:, b + o, :], w[:, H, d, c], w[:, L, d, c], src[:, H, d], src[:, L, d],
                                  first and d == 0, last and d == DT - 1, again)
                return ins

            def gather(b, xs, mh, ml, o):
                c = slice(o * P, (o + 1) * P)
                for t in range(NT):
                    ins = mm3(ps[:, b + o, :], xs[:, H, t, c], xs[:, L, t, c], mh[:, t], ml[:, t],
                              t == 0, t == NT - 1)
                return ins

            def gather_adj(b, xs):
                for o in range(DT):
                    mm(ps[:, b + o, :], xs[:, H, 0, o * P:(o + 1) * P], adjT[:, H, 0], start=True, stop=False)
                with pe.If(lo_words > 0):
                    for o in range(DT):
                        for t in range(NT):
                            mm(ps[:, b + o, :], xs[:, H, t, o * P:(o + 1) * P], adjT[:, L, t],
                               start=False, stop=False)
                for o in range(DT):
                    c = slice(o * P, (o + 1) * P)
                    for t in range(1, NT):
                        mm(ps[:, b + o, :], xs[:, H, t, c], adjT[:, H, t], start=False, stop=False)
                    for t in range(NT):
                        ins = mm(ps[:, b + o, :], xs[:, L, t, c], adjT[:, H, t], start=False, stop=t == NT - 1)
                return ins

            def to_natural(b, src, w):
                dst = natural(b)
                for t in range(NT):
                    c = slice(t * P, (t + 1) * P)
                    for d in range(DT):
                        ins = mm3(dst[:, t], src[:, H, d, c], src[:, L, d, c], w[:, H, d], w[:, L, d],
                                  d == 0, d == DT - 1)
                return ins

            def transpose_nodes(b, src):
                for d in range(DT):
                    for t in range(NT):
                        ins = nc.tensor.transpose(ps[:, b + d, t * P:(t + 1) * P], src[:, t, d * P:(d + 1) * P],
                                                  ident[:, :])
                return ins

            def transpose_features(b, src):
                dst = natural(b)
                for t in range(NT):
                    for d in range(DT):
                        ins = nc.tensor.transpose(dst[:, t, d * P:(d + 1) * P], src[:, d, t * P:(t + 1) * P],
                                                  ident[:, :])
                return ins

            pe.wait_ge(q_prep, 19)
            pe.wait_ge(q_pool, 5)
            for k, src in enumerate((stv0, st4, st3, st5, stu3, stu5)):
                for d in range(DT):
                    for o in range(DT):
                        ins = nc.tensor.transpose(ps[:, k, d * D + o * P:d * D + (o + 1) * P],
                                                  src[:, o, d * P:(d + 1) * P], ident[:, :])
                ins.then_inc(q_pe, 1)
            for d in range(DT):
                for e in range(DT):
                    ins = mm(ps[:, 6, d * D:(d + 1) * D], stq0[:, e, d * P:(d + 1) * P], stk0[:, e, :],
                             start=e == 0, stop=e == DT - 1)
            ins.then_inc(q_pe, 1)
            for j in range(PAIRS):
                ins = mm(ps[:, 7, 0:D], bvb[:, j, :], sto[:, j, :], start=j == 0, stop=j == PAIRS - 1)
            ins.then_inc(q_pe, 1)
            pe.wait_ge(q_prep, 33)
            for t in range(NT):
                for s in range(NT):
                    ins = nc.tensor.transpose(ps[:, t, s * P:(s + 1) * P], adj_n[:, s, t * P:(t + 1) * P],
                                              ident[:, :])
                ins.then_inc(q_pe, 1)
            pe.wait_ge(q_prep, 40)
            mm(ps[0:1, 7, 0:1], inexact[:, :], ones1[:, :], start=True, stop=True).then_inc(q_pe, 1)
            pe.wait_ge(q_prep, Q_PREP_ALL)
            lo_words = pe.value_load(any_lo[0:1, 0:1])

            def x_transposed(l, k):
                pe.wait_ge(x_in[l], 16 * k + 16)
                transpose_nodes(4 * l, XIN[l]).then_inc(xT_ps[l], 1)

            def y_of(l, k):
                pe.wait_ge(xT_l[l], k + 1)
                through(Y[l], W["g0"], HTS[l]).then_inc(y_ps[l], 1)

            for l in range(LANES):
                x_transposed(l, 0)
            for l in range(LANES):
                y_of(l, 0)

            with pe.Fori(0, ITERS) as it:
                v = it + 1

                def gram(l):
                    pe.wait_ge(y_l[l], v)
                    for t in range(NT):
                        c = slice(t * P, (t + 1) * P)
                        for d in range(DT):
                            ins = mm3(ps[:, 4 * l + t, :], HTS[l][:, H, d, c], HTS[l][:, L, d, c],
                                      AB[l][:, H, d], AB[l][:, L, d], d == 0, d == DT - 1)
                    ins.then_inc(s_ps[l], 1)

                def u_of(l, o):
                    if o == 0:
                        pe.wait_ge(rel_l[l], v)
                        pe.wait_ge(xs_l[l], v)
                    gather(4 * l, XNS[l], RELH[l], RELL[l], o).then_inc(u_ps[l], 1)

                def out_0(l):
                    pe.wait_ge(u_l[l], v)
                    to_natural(4 * l + 2, AB[l], W["wv0"]).then_inc(o_ps[l], 1)
                    pe.wait_ge(sq_s[l], it * (NT - 1) + (NT - 1))
                    for t in range(NT):
                        ins = mm(ps[:, 4 * l, t:t + 1], REL[l][:, 0, t * P:(t + 1) * P], ones1[:, :],
                                 start=True, stop=True)
                    ins.then_inc(ssq_ps[l], 1)

                def t_of(l):
                    pe.wait_ge(x1s_l[l], v)
                    gather_adj(4 * l, XNS[l]).then_inc(t_ps[l], 1)

                def out_1(l):
                    pe.wait_ge(t_l[l], v)
                    to_natural(4 * l + 2, AB[l], W["w1"]).then_inc(o1_ps[l], 1)

                def h_transposed(l, b):
                    pe.wait_ge(x2_r[l], v)
                    transpose_nodes(b, xn[:, l]).then_inc(hT_ps[l], 1)

                gram(0)
                gram(1)
                u_of(0, 0)
                u_of(0, 1)
                u_of(1, 0)
                out_0(0)
                u_of(1, 1)
                out_0(1)
                t_of(0)
                out_1(0)
                t_of(1)
                h_transposed(0, 0)
                out_1(1)
                def x3_transposed(l, b):
                    pe.wait_ge(x3_r[l], v)
                    transpose_nodes(b, xn[:, l]).then_inc(x3_ps[l], 1)

                for j in range(STEPS):
                    for l in range(LANES):
                        m = it * 6 + (j * 2 + l + 1)
                        o = 1 - l
                        pe.wait_ge(xn_l[l], it * 3 + (j + 1))
                        if l == 0 and j == 0:
                            pe.wait_ge(hT_l[0], it * 3 + 1)
                        gather_adj(0, XNS[l]).then_inc(a_ps, 1)
                        pe.wait_ge(hT_l[l], it * 3 + (j + 1))
                        pe.wait_ge(z_t, m)
                        through(2, W["u3"], HTS[l], last=False)
                        if j + l > 0:
                            pe.wait_ge(h_f[o], it * 4 + (j + 1 + l))
                            transpose_features(6, hT[o]).then_inc(tp_ps[o], 1)
                        pe.wait_ge(a_l, m)
                        through(2, W["w4"], AB[0], first=False).then_inc(r_ps, 1)
                        pe.wait_ge(v_t, m)
                        through(4, W["w5"], AB[0], last=False)
                        if l == 0 and j == 0:
                            h_transposed(1, 6)
                        pe.wait_ge(r_t, m)
                        through(2, W["wd"], AB[0], first=False, again=True).then_inc(z_ps, 1)
                        if l == 1 and j == STEPS - 1:
                            x3_transposed(0, 0)
                        pe.wait_ge(rh_l, m)
                        through(4, W["u5"], AB[1], first=False).then_inc(v_ps, 1)

                pe.wait_ge(x3_l[0], v)
                pe.wait_ge(z_t, it * 6 + 7)
                through(2, W["wq"], X3T).then_inc(q_ps[0], 1)
                pe.wait_ge(v_t, it * 6 + 7)
                through(4, W["wk"], X3T).then_inc(k_ps[0], 1)
                pe.wait_ge(h_f[1], it * 4 + 4)
                transpose_features(6, hT[1]).then_inc(tp_ps[1], 1)
                to_natural(0, X3T, W["wv"]).then_inc(vv_ps[0], 1)
                for n in range(-2, HEADJOBS + 1):
                    if n == -2:
                        pe.wait_ge(vv_l[0], v)
                    if n == -1:
                        pe.wait_ge(x3_l[1], v)
                        through(4, W["wq"], X3T).then_inc(q_ps[1], 1)
                        through(6, W["wk"], X3T).then_inc(k_ps[1], 1)
                    if n == 0:
                        pe.wait_ge(q_l[1], v)
                        pe.wait_ge(k_l[1], v)
                    if 0 <= n < HEADJOBS:
                        pe.wait_ge(nrm, it * QT + (n + 1) * NT)
                    s = n - 1
                    pr = s // 2
                    if n >= 1:
                        if s % 2 == 0 and pr % PAIRS >= 2:
                            pe.wait_ge(ot_l, it * (HEADJOBS // 2) + (pr - 1))
                        if s == HEADS:
                            pe.wait_ge(yo_r[0], v)
                            pe.wait_ge(vv_l[1], v)
                    if n == HEADS + 1:
                        pe.wait_ge(vv_l[1], v)
                    for k in range(NT):
                        if n >= 1 and k < NT - 1:
                            pe.wait_ge(pt_l, it * LT + (s * (NT - 1) + k + 1))
                        elif n >= 1:
                            pe.wait_ge(pt_h, it * QT + (s + 1) * NT)
                        if 0 <= n < HEADJOBS:
                            for q in range(NT):
                                ins = nc.tensor.transpose(ps[:, 4 + k, q * P:(q + 1) * P],
                                                          SC[:, (n * NT + q) % RING, k * P:(k + 1) * P],
                                                          ident[:, :])
                            ins.then_inc(pt_ps, 1)
                        if n >= 1:
                            w = VP[:, k * PAIRS + pr % PAIRS, s % 2, :]
                            dst = ps[:, 2 + pr % 2, :]
                            if k < NT - 1:
                                mm(dst, w, PT[:, 2 * k + H], start=s % 2 == 0 and k == 0, stop=False)
                                mm(dst, w, PT[:, 2 * k + L], start=False, stop=False).then_inc(pv, 1)
                            else:
                                mm(dst, f32(w), pt_whole[:, :], start=False, stop=s % 2 == 1).then_inc(pv, 1)
                        if n == -2 and k == 2:
                            x3_transposed(1, 6)
                        if n + 2 < HEADJOBS:
                            g = (n + 2) * NT + k
                            if k == 0:
                                slot = (n + 2) % 4
                                pe.wait_ge(stk[slot], it * (64 * HEADJOBS // 4) + 64 * ((n + 2) // 4 + 1))
                            pe.wait_ge(ttr, it * QT + (g + 1))
                            mm(ps[:, g % 2, :], STK[:, slot, 0, k * P:(k + 1) * P], STK[:, slot, 1, :],
                               start=True, stop=True).then_inc(sc_ps, 1)
                    if n == HEADS:
                        pe.wait_ge(ttr, it * QT + ((n + 3) * NT + 2))
                        to_natural(0, X3T, W["wv"]).then_inc(vv_ps[1], 1)
                    if n == HEADJOBS:
                        pe.wait_ge(ttr, it * QT + (QT + 2))
                        for l in range(LANES):
                            x_transposed(l, it + 1)
                    if n == HEADS or n == HEADJOBS:
                        l = n // HEADS - 1
                        pe.wait_ge(ot_l, it * (HEADJOBS // 2) + n // 2)
                        dst = natural(2)
                        for t in range(NT):
                            c = slice(t * P, (t + 1) * P)
                            for pr in range(PAIRS):
                                k = 2 * (pr % 2)
                                ins = mm3(dst[:, t], SRC[l][:, pr // 2, k + H, c], SRC[l][:, pr // 2, k + L, c],
                                          Wo[:, H, pr], Wo[:, L, pr], pr == 0, pr == PAIRS - 1)
                        ins.then_inc(yo_ps[l], 1)
                for l in range(LANES):
                    y_of(l, it + 1)


_INS = ["x", "adj", "L0_gnn_Wq", "L0_gnn_Wk", "L0_gnn_Wv", "L1_gnn_weight", "L1_gnn_bias",
        "L2_gnn_w3_w", "L2_gnn_w3_b", "L2_gnn_u3_w", "L2_gnn_u3_b", "L2_gnn_w4_w", "L2_gnn_w4_b",
        "L2_gnn_w5_w", "L2_gnn_w5_b", "L2_gnn_u5_w", "L2_gnn_u5_b",
        "L3_gnn_Wq", "L3_gnn_bq", "L3_gnn_Wk", "L3_gnn_bk", "L3_gnn_Wv", "L3_gnn_bv", "L3_gnn_Wo", "L3_gnn_bo"]


def kernel(**inputs):
    import concourse.bacc as bacc
    from concourse.bass_utils import run_bass_kernel_spmd

    nc = bacc.Bacc("TRN2", target_bir_lowering=False, num_devices=1)
    arrays, args = {}, []
    for name in _INS:
        a = np.ascontiguousarray(inputs[name])
        arrays[f"in_{name}"] = a
        args.append(nc.dram_tensor(f"in_{name}", a.shape, mybir.dt.from_np(a.dtype), kind="ExternalInput").ap())
    shape = tuple(inputs["x"].shape)
    args.append(nc.dram_tensor("out_0", shape, F32, kind="ExternalOutput").ap())
    gnn_stack(nc, *args)
    r = run_bass_kernel_spmd(nc, [arrays], core_ids=[0])
    return r.results[0]["out_0"]
```
